# Optimizing a Trainium2 kernel written in Bass

```python
import numpy as np
import jax
import jax.numpy as jnp

def _softmax(x, axis=-1):
    return jax.nn.softmax(x, axis=axis)

def _gelu(x):
    return jax.nn.gelu(x, approximate=True)

def _silu(x):
    return jax.nn.silu(x)

def _sigmoid(x):
    return jax.nn.sigmoid(x)

def _layernorm(x, axis=-1, eps=1e-05):
    m = jnp.mean(x, axis=axis, keepdims=True)
    v = jnp.var(x, axis=axis, keepdims=True)
    return (x - m) / jnp.sqrt(v + eps)

def _scatter_add(tgt, idx, src, axis=0):
    return tgt.at[idx].add(src)

def _segment_sum(src, seg, n):
    return jax.ops.segment_sum(src, seg, n)
kernel_name = 'mk_gnn_resnorm_d2_gnn_r8_b397a4'

def setup_inputs(seed: int=0):
    np.random.seed(seed)
    _w = jnp.asarray

    def _rec_inputs():
        import jax
        import jax.numpy as jnp
        _gk = jax.random.key(seed)
        x = -8.776e-05 + 1 * jax.random.normal(jax.random.fold_in(_gk, 1), (2500, 256), jnp.float32)
        src = jax.random.randint(jax.random.fold_in(_gk, 2), (80000,), 0, 2500, jnp.int32)
        dst = jax.random.randint(jax.random.fold_in(_gk, 3), (80000,), 0, 2500, jnp.int32)
        _o = jnp.argsort(dst, stable=True)
        src = src[_o]
        dst = dst[_o]
        edge_attr_64 = 0.000312547 + 1.00004 * jax.random.normal(jax.random.fold_in(_gk, 12), (80000, 64), jnp.float32)
        edge_type_8 = jax.random.randint(jax.random.fold_in(_gk, 14), (80000,), 0, 8, jnp.int32)
        return (x, src, dst, edge_attr_64, edge_type_8)
    x, src, dst, edge_attr_64, edge_type_8 = _rec_inputs()

    def _L0_gnn_setup():
        import jax, jax.numpy as jnp
        import numpy as np
        N_NODES = 2500
        N_EDGES = 37500
        D = 256
        NUM_RELS = 8
        NUM_BASES = 4
        key = jax.random.key(seed)
        ks = jax.random.split(key, 8)
        x = jax.random.normal(ks[0], (N_NODES, D), dtype=jnp.float32)
        src = jax.random.randint(ks[1], (N_EDGES,), 0, N_NODES, dtype=jnp.int32)
        dst = jax.random.randint(ks[2], (N_EDGES,), 0, N_NODES, dtype=jnp.int32)
        etypes = jax.random.randint(ks[3], (N_EDGES,), 0, NUM_RELS, dtype=jnp.int32)
        scale = 1.0 / np.sqrt(D)
        basis = jax.random.normal(ks[4], (NUM_BASES, D, D), dtype=jnp.float32) * scale
        comp = jax.random.normal(ks[5], (NUM_RELS, NUM_BASES), dtype=jnp.float32)
        loop_weight = jax.random.normal(ks[6], (D, D), dtype=jnp.float32) * scale
        bias_param = jnp.zeros((D,), dtype=jnp.float32)
        return {'x': x, 'src': src, 'dst': dst, 'etypes': etypes, 'basis': basis, 'comp': comp, 'loop_weight': loop_weight, 'bias_param': bias_param}
    _L0_gnn_all = _L0_gnn_setup()
    _L0_gnn_in = {k: v for k, v in _L0_gnn_all.items() if k in ('basis', 'comp', 'loop_weight', 'bias_param')}
    del _L0_gnn_all

    def _L1_gnn_setup():
        import jax, jax.numpy as jnp
        import numpy as np
        N, E, H, DE = (1250, 31250, 256, 64)
        EPS = 1e-05

        def _lin_init(k, fan_in, shape):
            s = 1.0 / np.sqrt(fan_in)
            return jax.random.uniform(k, shape, jnp.float32, -s, s)
        key = jax.random.key(seed)
        ks = jax.random.split(key, 12)
        x = jax.random.normal(ks[0], (N, H), jnp.float32)
        edge_index = jax.random.randint(ks[1], (2, E), 0, N)
        edge_attr = jax.random.normal(ks[2], (E, DE), jnp.float32)
        d_in = H + DE
        W1 = _lin_init(ks[3], d_in, (d_in, H))
        b1 = _lin_init(ks[4], d_in, (H,))
        W2 = _lin_init(ks[5], H, (H, H))
        b2 = _lin_init(ks[6], H, (H,))
        Wg = _lin_init(ks[7], d_in, (d_in, H))
        bg = _lin_init(ks[8], d_in, (H,))
        gamma = jnp.ones((H,), jnp.float32)
        beta = jnp.zeros((H,), jnp.float32)
        return {'x': x, 'edge_index': edge_index, 'edge_attr': edge_attr, 'W1': W1, 'b1': b1, 'W2': W2, 'b2': b2, 'Wg': Wg, 'bg': bg, 'gamma': gamma, 'beta': beta}
    _L1_gnn_all = _L1_gnn_setup()
    _L1_gnn_in = {k: v for k, v in _L1_gnn_all.items() if k in ('W1', 'b1', 'W2', 'b2', 'Wg', 'bg', 'gamma', 'beta')}
    del _L1_gnn_all
    return {'x': x, 'src': src, 'dst': dst, 'edge_attr_64': edge_attr_64, 'edge_type_8': edge_type_8, 'L0_gnn_basis': _L0_gnn_in['basis'], 'L0_gnn_comp': _L0_gnn_in['comp'], 'L0_gnn_loop_weight': _L0_gnn_in['loop_weight'], 'L0_gnn_bias_param': _L0_gnn_in['bias_param'], 'L1_gnn_W1': _L1_gnn_in['W1'], 'L1_gnn_b1': _L1_gnn_in['b1'], 'L1_gnn_W2': _L1_gnn_in['W2'], 'L1_gnn_b2': _L1_gnn_in['b2'], 'L1_gnn_Wg': _L1_gnn_in['Wg'], 'L1_gnn_bg': _L1_gnn_in['bg'], 'L1_gnn_gamma': _L1_gnn_in['gamma'], 'L1_gnn_beta': _L1_gnn_in['beta']}

def reference(x, src, dst, edge_attr_64, edge_type_8, L0_gnn_basis, L0_gnn_comp, L0_gnn_loop_weight, L0_gnn_bias_param, L1_gnn_W1, L1_gnn_b1, L1_gnn_W2, L1_gnn_b2, L1_gnn_Wg, L1_gnn_bg, L1_gnn_gamma, L1_gnn_beta):
    import jax
    import jax.numpy as jnp

    def _L0_gnn_ref(x, src, dst, etypes, basis, comp, loop_weight, bias_param):
        import jax, jax.numpy as jnp
        import numpy as np
        N_NODES = 2500
        N_EDGES = 37500
        D = 256
        NUM_RELS = 8
        NUM_BASES = 4
        W = jnp.einsum('rb,bio->rio', comp, basis)
        H = jnp.einsum('ni,rio->nro', x, W)
        msg = H[src, etypes]
        agg = jax.ops.segment_sum(msg, dst, num_segments=N_NODES)
        out = agg + x @ loop_weight + bias_param
        return out

    def _L1_gnn_ref(x, edge_index, edge_attr, W1, b1, W2, b2, Wg, bg, gamma, beta):
        import jax, jax.numpy as jnp
        import numpy as np
        N, E, H, DE = (1250, 31250, 256, 64)
        EPS = 1e-05

        def _lin_init(k, fan_in, shape):
            s = 1.0 / np.sqrt(fan_in)
            return jax.random.uniform(k, shape, jnp.float32, -s, s)
        src, dst = (edge_index[0], edge_index[1])
        ei = jnp.concatenate([x[src], edge_attr], axis=-1)
        core = jnp.maximum(ei @ W1 + b1, 0.0) @ W2 + b2
        gate = jax.nn.sigmoid(ei @ Wg + bg)
        msg = gate * core
        agg = jax.ops.segment_sum(msg, dst, num_segments=x.shape[0])
        out = agg + x
        mu = jnp.mean(out, axis=-1, keepdims=True)
        var = jnp.var(out, axis=-1, keepdims=True)
        out = (out - mu) * jax.lax.rsqrt(var + EPS) * gamma + beta
        return out
    edge_index = jnp.stack([src, dst])
    x = _layernorm(x + _L0_gnn_ref(x, src, dst, edge_type_8, L0_gnn_basis, L0_gnn_comp, L0_gnn_loop_weight, L0_gnn_bias_param), axis=-1)
    x = _layernorm(x + _L1_gnn_ref(x, edge_index, edge_attr_64, L1_gnn_W1, L1_gnn_b1, L1_gnn_W2, L1_gnn_b2, L1_gnn_Wg, L1_gnn_bg, L1_gnn_gamma, L1_gnn_beta), axis=-1)
    return x

_drawn_inputs = setup_inputs


def setup_inputs(seed=0):
    import zlib

    import numpy as np

    out = dict(_drawn_inputs(seed))
    spreads = {'L0_gnn_bias_param': (0.0, 0.8), 'L1_gnn_gamma': (1.0, 0.2), 'L1_gnn_beta': (0.0, 0.1)}
    factors = {'L1_gnn_bg': 7.162}
    for name, (base, spread) in spreads.items():
        noise = np.random.default_rng([zlib.crc32(name.encode()), seed]).standard_normal(out[name].shape)
        drawn = base * np.exp(spread * noise) if base else spread * noise
        out[name] = jnp.asarray(drawn.astype(out[name].dtype))
    for name, factor in factors.items():
        out[name] = (out[name] * factor).astype(out[name].dtype)
    return out
```

```python
from contextlib import ExitStack

import concourse.bass as bass
from concourse import mybir

F32 = mybir.dt.float32
F32R = mybir.dt.float32r
I32 = mybir.dt.int32
ALU = mybir.AluOpType
ACT = mybir.ActivationFunctionType
AX = mybir.AxisListType

P = 128
GROUP = 5
WIN = 32
NODE_TILE = 125
EPS = 1e-5


def build(nc, x, xT, src, dst, etype, edge_T, basis, comp, loop_w, bias0,
          W1, b1, W2, b2, Wg, bg, gamma, beta, out):
    N, D = x.shape
    G = src.shape[0]
    TILES = G * GROUP
    DE = edge_T.shape[0]
    NB, NR = basis.shape[0], comp.shape[0]
    C = D // P
    NT = N // NODE_TILE
    PAIRS = G // 2
    NWIN = 2 * -(-N // (2 * WIN))
    NPAD = NWIN * WIN
    KB = C * NB
    assert G % 2 == 1 and NT * NODE_TILE == N and NT % 2 == 0 and 2 * DE == P and KB == 8
    GE = GROUP * P

    h_table = nc.dram_tensor("node_table", [N, 2 * D], F32, kind="Internal").ap()
    x1_dram = nc.dram_tensor("x1_rows", [N, D], F32, kind="Internal").ap()

    ctx = ExitStack()
    with ctx:
        def sb(name, shape, dt=F32):
            return ctx.enter_context(nc.sbuf_tensor(name, shape, dt))

        def sem(name):
            return ctx.enter_context(nc.semaphore(name))

        bank = [ctx.enter_context(nc.psum_tensor(f"bank{i}", [P, 512], F32)) for i in range(8)]

        ident = sb("ident", [P, P])
        iota = sb("iota", [P, NPAD])
        ones_r = sb("ones_r", [64, P], F32R)
        zero = sb("zero", [P, 1])
        dst_f = sb("dst_f", [P, TILES])
        typ_f = sb("typ_f", [P, TILES])
        src_slot = sb("src_slot", [P, 2, GROUP], I32)
        ext = sb("ext", [P, 2, P])
        ext2 = sb("ext2", [P, 4])
        ext_wide = sb("ext_wide", [P, 2, P])
        base_row = sb("base_row", [1, P], I32)
        span_f = sb("span_f", [1, 2])
        span_i = sb("span_i", [1, 2], I32)
        basis_sb = sb("basis_sb", [P, KB, D])
        loop_sb = sb("loop_sb", [P, C, D])
        comp_bc = sb("comp_bc", [P, NR * NB])
        comp_T = sb("comp_T", [P, NB, NR])
        bias0_bc = sb("bias0_bc", [P, D])
        wx = sb("wx", [P, C, 2 * D])
        bx_bc = sb("bx_bc", [P, 2 * D])
        we = sb("we", [P, 2 * D])
        we_hi = sb("we_hi", [P, 2 * D], F32R)
        we_lo = sb("we_lo", [P, 2 * D], F32R)
        w2 = sb("w2", [P, C, D])
        w2_hi = sb("w2_hi", [P, C, D], F32R)
        w2_lo = sb("w2_lo", [P, C, D], F32R)
        b2_two = sb("b2_two", [64, D])
        b2_r = sb("b2_r", [64, D], F32R)
        gamma_bc = sb("gamma_bc", [P, D])
        beta_bc = sb("beta_bc", [P, D])
        rows = sb("rows", [P, 2 * GROUP, 2 * D])
        sumT0 = sb("sumT0", [P, KB, NPAD])
        sumT1 = sb("sumT1", [P, C, NPAD])
        type_hot = sb("type_hot", [P, GROUP, NR])
        comp_prod = sb("comp_prod", [P, GROUP, NB, NR])
        comp_e = sb("comp_e", [P, 2, GROUP, NB])
        hot = sb("hot", [P, 2, GROUP, WIN])
        whot = sb("whot", [P, 2, GROUP, NB, WIN])
        edge_f = sb("edge_f", [P, 2, GE])
        edge_r = sb("edge_r", [P, 2, GE], F32R)
        h_hi = sb("h_hi", [P, 2, D], F32R)
        h_lo = sb("h_lo", [P, 2, D], F32R)
        msg = sb("msg", [P, 2 * GROUP, D])
        iota_i = msg[:, :, :].rearrange("p t n -> p (t n)").bitcast(I32)
        edge_words = edge_f[:, :, :].rearrange("p q n -> p (q n)").bitcast(I32)
        dst_i, typ_i = edge_words[:, 0:TILES], edge_words[:, TILES:2 * TILES]
        assert NPAD == 2 * GROUP * D and 2 * TILES <= 2 * GE
        rows_flat = rows[:, :, :].rearrange("p t n -> p (t n)")
        cuts = [0]

        def cut(*shape):
            size = 1
            for n in shape:
                size *= n
            cuts.append(cuts[-1] + size)
            assert cuts[-1] <= 4 * GROUP * D
            return rows_flat[:, cuts[-2]:cuts[-1]]

        stage = cut(2, KB, NODE_TILE).rearrange("p (q k n) -> p q k n", q=2, k=KB)
        table_s = cut(2, 2 * D).rearrange("p (q n) -> p q n", q=2)
        y = cut(2, D).rearrange("p (q n) -> p q n", q=2)
        y2 = cut(2, D).rearrange("p (q n) -> p q n", q=2)
        x1_s = cut(2, D).rearrange("p (q n) -> p q n", q=2)
        x1T = cut(2, C, NODE_TILE).rearrange("p (q c n) -> p q c n", q=2, c=C)
        xT_s = sb("xT_s", [P, 2, C, NODE_TILE])
        x_s = sb("x_s", [P, 2, D])
        stats = sb("stats", [P, 2, 6])
        mv = sb("mv", [P, 2, 2])
        std = sb("std", [P, 2, 1])
        rstd = sb("rstd", [P, 2, 1])
        eps = sb("eps", [P, 1])

        ident_set, iota_set, consts = sem("ident_set"), sem("iota_set"), sem("consts")
        edges_in, weights_in, b2_in = sem("edges_in"), sem("weights_in"), sem("b2_in")
        pool_zeroed, floats_ready, iota_ready = sem("pool_zeroed"), sem("floats_ready"), sem("iota_ready")
        ext_ready, ext_turned, ext2_ready, span_ready, wide_ready, plan_wide, widest_ready, plan_ready = (
            sem("ext_ready"), sem("ext_turned"), sem("ext2_ready"), sem("span_ready"), sem("wide_ready"),
            sem("plan_wide"), sem("widest_ready"), sem("plan_ready"))
        sums_zero, comp_turned, split_w, w_hi = sem("sums_zero"), sem("comp_turned"), sem("split_w"), sem("w_hi")
        src0_in = [sem(f"src0_in{q}") for q in range(2)]
        x_in = [sem(f"x_in{q}") for q in range(2)]
        x_used = sem("x_used")
        type_hot_ready, comp_prod_ready, comp_e_ready = (
            sem("type_hot_ready"), sem("comp_prod_ready"), sem("comp_e_ready"))
        hot0_ready, whot_ready, sum0_ready, sum0_added, layer0_summed = (
            sem("hot0_ready"), sem("whot_ready"), sem("sum0_ready"), sem("sum0_added"), sem("layer0_summed"))
        node_in = [sem(f"node_in{q}") for q in range(2)]
        staged, mixed, mix_used, y_ready, stats_ready, var_ready, std_ready, rstd_ready = (
            sem("staged"), sem("mixed"), sem("mix_used"), sem("y_ready"), sem("stats_ready"), sem("var_ready"),
            sem("std_ready"), sem("rstd_ready"))
        x1_ready, x1_turned, x1T_ready = sem("x1_ready"), sem("x1_turned"), sem("x1T_ready")
        table_mm, table_ready = sem("table_mm"), sem("table_ready")
        x1_out, table_out = [sem(f"x1_out{q}") for q in range(2)], [sem(f"table_out{q}") for q in range(2)]
        src1_in = [sem(f"src1_in{q}") for q in range(2)]
        edge_in = [sem(f"edge_in{q}") for q in range(2)]
        edge_hi, edge_split = sem("edge_hi"), sem("edge_split")
        row_in = [sem(f"row_in{q}") for q in range(2)]
        z_ready, pre_ready, gate_ready, turned = (
            sem("z_ready"), sem("pre_ready"), sem("gate_ready"), sem("turned"))
        hi_ready, lo_ready, core_ready, msg_ready = (
            sem("hi_ready"), sem("lo_ready"), sem("core_ready"), sem("msg_ready"))
        hot1_ready, sum1_ready, sum1_added, layer1_summed = (
            sem("hot1_ready"), sem("sum1_ready"), sem("sum1_added"), sem("layer1_summed"))
        x1_in = [sem(f"x1_in{q}") for q in range(2)]
        sum_staged, sum_turned = sem("sum_staged"), sem("sum_turned")
        f_sum, f_stats, f_var, f_std, f_rstd, f_norm, f_scaled, f_shifted, f_res = (
            sem(f"f_{s}") for s in ("sum", "stats", "var", "std", "rstd", "norm", "scaled", "shifted", "res"))
        out_ready, passed = sem("out_ready"), sem("passed")
        out_done = [sem(f"out_done{q}") for q in range(2)]

        def static(v):
            return isinstance(v, int)

        def pairs(eng, step):
            step(0, 0, 0)
            step(1, 1, 0)
            with eng.Fori(1, PAIRS) as i:
                step(0, 2 * i, i)
                step(1, 2 * i + 1, i)
            step(0, G - 1, PAIRS)

        def node_pairs(eng, step):
            step(0, 0, 0)
            step(1, 1, 0)
            with eng.Fori(1, NT // 2 - 1) as i:
                step(0, 2 * i, i)
                step(1, 2 * i + 1, i)
            step(0, NT - 2, NT // 2 - 1)
            step(1, NT - 1, NT // 2 - 1)

        def ticks(eng, tick):
            for k in range(2 * GROUP):
                tick(k, 0)
            with eng.Fori(1, PAIRS) as i:
                for k in range(2 * GROUP):
                    tick(k, i)
            for k in range(2 * GROUP):
                tick(k, PAIRS)

        def tile_at(k, i, lag):
            if static(i) and not 0 <= 2 * GROUP * i + k - lag < TILES:
                return None
            return 2 * GROUP * i + (k - lag), (k - lag) % (2 * GROUP), (k - lag) % 2

        def group_at(k, i, lag):
            at = tile_at(k, i, lag)
            if at is None or (k - lag) % GROUP:
                return None
            return 2 * i + (k - lag) // GROUP, ((k - lag) // GROUP) % 2

        def settle(eng):
            eng.sem_inc(passed, 1)

        def nodes(n):
            return bass.ds(n * NODE_TILE, NODE_TILE)

        block = ctx.enter_context(nc.Block())

        @block.sync
        def _(sp):
            sp.dma_start(dst_i, dst).then_inc(edges_in, 16)
            sp.dma_start(typ_i, etype).then_inc(edges_in, 16)
            sp.dma_start(comp_bc[:, :],
                         comp.rearrange("(o r) b -> o (r b)", o=1).to_broadcast([P, NR * NB])).then_inc(edges_in, 16)

            def load_src0(q, g, i):
                if not (static(g) and g < 2):
                    sp.wait_ge(x_in[q], 16 * GROUP * i)
                sp.dma_start(src_slot[:, q, :], src[g, :, :]).then_inc(src0_in[q], 16)

            pairs(sp, load_src0)

            def load_nodes(q, n):
                sp.dma_start(xT_s[:, q, :, :], xT[:, :, nodes(n)]).then_inc(node_in[q], 16)
                sp.dma_start(x_s[0:NODE_TILE, q, :], x[nodes(n), :]).then_inc(node_in[q], 16)

            def node_tile(q, n, i):
                sp.wait_ge(x1_ready, n + 1)
                sp.dma_start(x1_dram[nodes(n), :], x1_s[0:NODE_TILE, q, :]).then_inc(x1_out[q], 16)
                if not (static(n) and n >= NT - 2):
                    sp.wait_ge(mixed, n + 1)
                    sp.wait_ge(mix_used, n + 1)
                    load_nodes(q, n + 2)
                sp.wait_ge(table_ready, n + 1)
                sp.dma_start(h_table[nodes(n), :], table_s[0:NODE_TILE, q, :]).then_inc(table_out[q], 16)

            load_nodes(0, 0)
            load_nodes(1, 1)
            node_pairs(sp, node_tile)

            def load_edges(q, g, i):
                if not (static(g) and g < 2):
                    sp.wait_ge(row_in[q], 16 * GROUP * i)
                sp.dma_start(src_slot[:, q, :], src[g, :, :]).then_inc(src1_in[q], 16)
                if not (static(g) and g < 2):
                    sp.wait_ge(edge_split, g - 1)
                for half in range(2):
                    sp.dma_start(edge_f[half * DE:(half + 1) * DE, q, :],
                                 edge_T[:, bass.ds(g * GE, GE)]).then_inc(edge_in[q], 16)

            sp.wait_ge(x_in[0], 16 * GROUP * (PAIRS + 1))
            sp.wait_ge(x_in[1], 16 * GROUP * PAIRS)
            pairs(sp, load_edges)

            for q in range(2):
                sp.wait_ge(x1_out[q], 16 * (NT // 2))

            def load_x1(q, n):
                sp.dma_start(x_s[0:NODE_TILE, q, :], x1_dram[nodes(n), :]).then_inc(x1_in[q], 16)

            def out_tile(q, n, i):
                sp.wait_ge(out_ready, n + 1)
                sp.dma_start(out[nodes(n), :], x1_s[0:NODE_TILE, q, :]).then_inc(out_done[q], 16)
                if not (static(n) and n >= NT - 2):
                    load_x1(q, n + 2)

            sp.wait_ge(mix_used, NT)
            load_x1(0, 0)
            load_x1(1, 1)
            node_pairs(sp, out_tile)
            for q in range(2):
                sp.wait_ge(out_done[q], 16 * (NT // 2))

        @block.gpsimd
        def _(pool):
            pool.memset(ident[:, :], 0.0).then_inc(pool_zeroed, 1)
            pool.iota(iota_i, [[1, NPAD]], base=0, channel_multiplier=0).then_inc(iota_set, 1)
            pool.wait_ge(pool_zeroed, 1)
            pool.affine_select(out=ident[:, :], in_=ident[:, :], compare_op=ALU.not_equal, fill=1.0,
                               base=0, pattern=[[-1, P]], channel_multiplier=1).then_inc(ident_set, 1)

            def gather_x(q, g, i):
                pool.wait_ge(src0_in[q], 16 * (i + 1))
                if not (static(g) and g < 2):
                    pool.wait_ge(x_used, g - 1)
                settle(pool)
                for j in range(GROUP):
                    pool.indirect_dma_start(
                        out=rows[:, q * GROUP + j, 0:D], out_offset=None, in_=x,
                        in_offset=bass.IndirectOffsetOnAxis(ap=src_slot[:, q, j:j + 1], axis=0)).then_inc(x_in[q], 16)

            pairs(pool, gather_x)

            def gather_rows(q, g, i):
                pool.wait_ge(src1_in[q], 16 * (i + 1))
                if not (static(g) and g < 2):
                    pool.wait_ge(msg_ready, GROUP * (g - 1))
                settle(pool)
                for j in range(GROUP):
                    pool.indirect_dma_start(
                        out=rows[:, q * GROUP + j, :], out_offset=None, in_=h_table,
                        in_offset=bass.IndirectOffsetOnAxis(ap=src_slot[:, q, j:j + 1], axis=0)).then_inc(row_in[q], 16)

            for q in range(2):
                pool.wait_ge(table_out[q], 16 * (NT // 2))
                pool.wait_ge(x1_out[q], 16 * (NT // 2))
            pool.wait_ge(x_used, G)
            pairs(pool, gather_rows)

        @block.scalar
        def _(act):
            def row(v, n):
                return v.rearrange("(o n) -> o n", o=1).to_broadcast([P, n])

            for to, at in [
                (basis_sb[:, 0:NB, :], basis[:, 0:P, :].rearrange("b p n -> p b n")),
                (basis_sb[:, NB:KB, :], basis[:, P:D, :].rearrange("b p n -> p b n")),
                (loop_sb[:, :, :], loop_w.rearrange("(c p) n -> p c n", p=P)),
                (bias0_bc[:, :], row(bias0, D)),
                (wx[:, :, 0:D], W1[0:D, :].rearrange("(c p) n -> p c n", p=P)),
                (wx[:, :, D:2 * D], Wg[0:D, :].rearrange("(c p) n -> p c n", p=P)),
                (bx_bc[:, 0:D], row(b1, D)),
                (bx_bc[:, D:2 * D], row(bg, D)),
                (we[0:DE, 0:D], W1[D:D + DE, :]),
                (we[DE:P, 0:D], W1[D:D + DE, :]),
                (we[0:DE, D:2 * D], Wg[D:D + DE, :]),
                (we[DE:P, D:2 * D], Wg[D:D + DE, :]),
                (w2[:, :, :], W2.rearrange("(c p) n -> p c n", p=P)),
                (gamma_bc[:, :], row(gamma, D)),
                (beta_bc[:, :], row(beta, D)),
            ]:
                act.dma_start(to, at).then_inc(weights_in, 16)
            act.wait_ge(consts, 4)
            b2_row = b2.rearrange("(o n) -> o n", o=1)
            act.dma_start(b2_two[0:1, :], b2_row).then_inc(b2_in, 16)
            act.dma_start(b2_two[32:33, :], b2_row).then_inc(b2_in, 16)
            for sums, k in [(sumT0, k) for k in range(KB)] + [(sumT1, c) for c in range(C)]:
                act.activation(sums[:, k, :], zero[:, 0:1].to_broadcast([P, NPAD]), ACT.Copy).then_inc(sums_zero, 1)

            act.wait_ge(layer0_summed, 1)

            def stage_sums(q, n):
                act.activation(stage[:, q, :, :], sumT0[:, :, nodes(n)], ACT.Copy).then_inc(staged, 1)

            def node_tile(q, n, i):
                act.wait_ge(var_ready, n + 1)
                act.activation(std[0:NODE_TILE, q, :], mv[0:NODE_TILE, q, 1:2], ACT.Sqrt,
                               bias=eps[0:NODE_TILE, 0:1]).then_inc(std_ready, 1)
                act.wait_ge(mixed, n + 1)
                if not (static(n) and n >= NT - 2):
                    stage_sums(q, n + 2)
                act.wait_ge(x1_turned, n + 1)
                if not (static(n) and n < 2):
                    act.wait_ge(table_mm, n - 1)
                act.activation(x1T[:, q, :, :].rearrange("p c n -> p (c n)"), bank[2 + q][:, 0:C * NODE_TILE],
                               ACT.Copy).then_inc(x1T_ready, 1)

            stage_sums(0, 0)
            stage_sums(1, 1)
            node_pairs(act, node_tile)

            def split_hi(g, q, i):
                act.wait_ge(edge_in[q], 32 * (i + 1))
                if not (static(g) and g < 2):
                    act.wait_ge(z_ready, GROUP * (g - 1))
                act.activation(edge_r[:, q, :], edge_f[:, q, :], ACT.Copy).then_inc(edge_hi, 1)

            split_hi(0, 0, 0)

            def tick(k, i):
                if at := group_at(k, i, -3):
                    split_hi(*at, i + (k + 3) // (2 * GROUP))
                if at := tile_at(k, i, 0):
                    t, ten, two = at
                    act.wait_ge(pre_ready, t + 1)
                    act.activation(rows[:, ten, D:2 * D], rows[:, ten, D:2 * D], ACT.Sigmoid).then_inc(gate_ready, 1)
                if at := tile_at(k, i, 1):
                    t, ten, two = at
                    act.wait_ge(turned, t + 1)
                    if not (static(t) and t < 2):
                        act.wait_ge(core_ready, t - 1)
                    act.activation(h_hi[:, two, :], bank[2 + two][:, 0:D], ACT.Relu).then_inc(hi_ready, 1)

            ticks(act, tick)

            act.wait_ge(layer1_summed, 1)

            def stage_sum1(q, n):
                act.activation(stage[:, q, 0:C, :], sumT1[:, :, nodes(n)], ACT.Copy).then_inc(sum_staged, 1)

            def out_tile(q, n, i):
                for h in range(2):
                    act.wait_ge(f_var, 2 * n + 1 + h)
                    act.activation(std[0:NODE_TILE, q, :], mv[0:NODE_TILE, q, 1:2], ACT.Sqrt,
                                   bias=eps[0:NODE_TILE, 0:1]).then_inc(f_std, 1)
                if not (static(n) and n >= NT - 2):
                    act.wait_ge(sum_turned, n + 1)
                    stage_sum1(q, n + 2)

            stage_sum1(0, 0)
            stage_sum1(1, 1)
            node_pairs(act, out_tile)

        @block.tensor
        def _(pe):
            pe.wait_ge(ident_set, 1)
            pe.wait_ge(ext_ready, 2)
            for s in range(2):
                pe.transpose(bank[s][0:G, 0:P], ext[:, s, 0:G], ident[:, :]).then_inc(ext_turned, 1)
            pe.wait_ge(wide_ready, 2)
            for s in range(2):
                pe.matmul(bank[2 + s][:, 0:G], ext_wide[0:G, s, :], ident[0:G, 0:G]).then_inc(plan_wide, 1)
            pe.wait_ge(plan_ready, 2)
            widest = pe.value_load(span_i[0:1, 0:1], min_val=0, max_val=N)

            def group_sums(rhs, lhs, to, width):
                for c in range(C):
                    for j in range(GROUP):
                        last = pe.matmul(to[:, c * width:(c + 1) * width], lhs(j, c), rhs(j),
                                         start=(j == 0), stop=(j == GROUP - 1))
                return last

            def layer0(windows):
                def step(q, slot, s, first):
                    pe.wait_ge(whot_ready, s + 1)
                    if not first:
                        pe.wait_ge(sum0_added, s - 1)
                    return group_sums(lambda j: whot[:, slot, j, :, :].rearrange("p b w -> p (b w)"),
                                      lambda j, c: rows[:, q * GROUP + j, c * P:(c + 1) * P],
                                      bank[6 + slot], NB * WIN).then_inc(sum0_ready, 1)

                def group(q, g, i):
                    pe.wait_ge(x_in[q], 16 * GROUP * (i + 1))
                    if windows == 1:
                        step(q, q, g, static(g) and g < 2)
                        return
                    first = static(g) and g == 0
                    settle(pe)
                    if first:
                        for w in range(2):
                            step(q, w, w, True)
                    with pe.Fori(1 if first else 0, windows // 2 - 1) as w:
                        for v in range(2):
                            step(q, v, g * windows + 2 * w + v, False)
                    step(q, 0, g * windows + windows - 2, False)
                    step(q, 1, g * windows + windows - 1, False)

                pairs(pe, group)

            with pe.If(widest < WIN):
                layer0(1)
            with pe.Else():
                layer0(NWIN)

            pe.wait_ge(weights_in, 16 * 15)

            def mix(q, n, i):
                pe.wait_ge(staged, n + 1)
                pe.wait_ge(node_in[q], 32 * (i + 1))
                if not (static(n) and n < 2):
                    pe.wait_ge(mix_used, n - 1)
                for k in range(KB):
                    pe.matmul(bank[q][0:NODE_TILE, 0:D], stage[:, q, k, :], basis_sb[:, k, :],
                              start=(k == 0), stop=False)
                for c in range(C):
                    last = pe.matmul(bank[q][0:NODE_TILE, 0:D], xT_s[:, q, c, :], loop_sb[:, c, :],
                                     start=False, stop=(c == C - 1))
                last.then_inc(mixed, 1)

            def node_tile(q, n, i):
                if not (static(n) and n >= NT - 1):
                    mix(1 - q, n + 1, i + q)
                pe.wait_ge(x1_ready, n + 1)
                if not (static(n) and n < 2):
                    pe.wait_ge(x1T_ready, n - 1)
                for c in range(C):
                    last = pe.transpose(bank[2 + q][:, c * NODE_TILE:(c + 1) * NODE_TILE],
                                        x1_s[0:NODE_TILE, q, c * P:(c + 1) * P], ident[0:NODE_TILE, 0:NODE_TILE])
                last.then_inc(x1_turned, 1)
                pe.wait_ge(x1T_ready, n + 1)
                if not (static(n) and n < 2):
                    pe.wait_ge(table_ready, n - 1)
                for c in range(C):
                    last = pe.matmul(bank[4 + q][0:NODE_TILE, :], x1T[:, q, c, :], wx[:, c, :],
                                     start=(c == 0), stop=(c == C - 1))
                last.then_inc(table_mm, 1)

            mix(0, 0, 0)
            node_pairs(pe, node_tile)

            pe.wait_ge(split_w, 6)

            def layer1(windows):
                def step(q, slot, s, first):
                    pe.wait_ge(hot1_ready, s + 1)
                    if not first:
                        pe.wait_ge(sum1_added, s - 1)
                    return group_sums(lambda j: hot[:, slot, j, :],
                                      lambda j, c: msg[:, q * GROUP + j, c * P:(c + 1) * P],
                                      bank[6 + slot], WIN).then_inc(sum1_ready, 1)

                def tick(k, i):
                    if at := tile_at(k, i, 0):
                        t, ten, two = at
                        if at := group_at(k, i, 0):
                            pe.wait_ge(edge_split, at[0] + 1)
                        if not (static(t) and t < 2):
                            pe.wait_ge(pre_ready, t - 1)
                        lhs = edge_r[:, ten // GROUP, (ten % GROUP) * P:(ten % GROUP + 1) * P]
                        pe.matmul(bank[two][:, :], lhs, we_hi[:, :], start=True, stop=False)
                        pe.matmul(bank[two][:, :], lhs, we_lo[:, :], start=False, stop=True).then_inc(z_ready, 1)
                    if at := tile_at(k, i, 1):
                        t, ten, two = at
                        pe.wait_ge(pre_ready, t + 1)
                        if not (static(t) and t < 2):
                            pe.wait_ge(lo_ready, t - 1)
                        for c in range(C):
                            last = pe.transpose(bank[2 + two][:, c * P:(c + 1) * P],
                                                rows[:, ten, c * P:(c + 1) * P], ident[:, :])
                        last.then_inc(turned, 1)
                    if at := tile_at(k, i, 2):
                        t, ten, two = at
                        pe.wait_ge(lo_ready, t + 1)
                        if not (static(t) and t < 2):
                            pe.wait_ge(msg_ready, t - 1)
                        to = bank[4 + two][:, 0:D]
                        pe.matmul(to, ones_r[:, :], b2_r[:, :], start=True, stop=False)
                        for c in range(C):
                            part = slice(c * P, (c + 1) * P)
                            pe.matmul(to, h_hi[:, two, part], w2_hi[:, c, :], start=False, stop=False)
                            pe.matmul(to, h_hi[:, two, part], w2_lo[:, c, :], start=False, stop=False)
                            last = pe.matmul(to, h_lo[:, two, part], w2_hi[:, c, :], start=False, stop=(c == C - 1))
                        last.then_inc(core_ready, 1)
                    if at := group_at(k, i, 8):
                        g, q = at
                        pe.wait_ge(msg_ready, GROUP * (g + 1))
                        if windows == 1:
                            step(q, q, g, static(g) and g < 2)
                        else:
                            first = static(g) and g == 0
                            settle(pe)
                            if first:
                                for w in range(2):
                                    step(q, w, w, True)
                            with pe.Fori(1 if first else 0, windows // 2 - 1) as w:
                                for v in range(2):
                                    step(q, v, g * windows + 2 * w + v, False)
                            step(q, 0, g * windows + windows - 2, False)
                            step(q, 1, g * windows + windows - 1, False)

                ticks(pe, tick)

            with pe.If(widest < WIN):
                layer1(1)
            with pe.Else():
                layer1(NWIN)

            def out_tile(q, n, i):
                pe.wait_ge(sum_staged, n + 1)
                if not (static(n) and n < 2):
                    pe.wait_ge(f_sum, n - 1)
                for c in range(C):
                    last = pe.transpose(bank[2 + q][0:NODE_TILE, c * P:(c + 1) * P], stage[:, q, c, :], ident[:, :])
                last.then_inc(sum_turned, 1)

            node_pairs(pe, out_tile)

        @block.vector
        def _(dve):
            dve.memset(zero[:, :], 0.0).then_inc(consts, 1)
            dve.memset(b2_two[:, :], 0.0).then_inc(consts, 1)
            dve.memset(ones_r[:, :].bitcast(F32), 1.0).then_inc(consts, 1)
            dve.memset(eps[:, :], EPS).then_inc(consts, 1)
            dve.wait_ge(edges_in, 48)
            dve.tensor_copy(dst_f[:, :], dst_i).then_inc(floats_ready, 1)
            dve.tensor_copy(typ_f[:, :], typ_i).then_inc(floats_ready, 1)
            dve.tensor_copy(comp_T[:, :, :], comp_bc[:, :].rearrange("p (r b) -> p b r", r=NR)).then_inc(comp_turned, 1)
            dve.wait_ge(floats_ready, 2)
            by_group = dst_f[:, :].rearrange("p (g j) -> p g j", j=GROUP)
            dve.tensor_reduce(ext[:, 0, 0:G], by_group, AX.X, ALU.min).then_inc(ext_ready, 1)
            dve.tensor_reduce(ext[:, 1, 0:G], by_group, AX.X, ALU.max).then_inc(ext_ready, 1)
            dve.wait_ge(ext_turned, 2)
            dve.tensor_reduce(ext2[0:G, 0:1], bank[0][0:G, 0:P], AX.X, ALU.min).then_inc(ext2_ready, 1)
            dve.tensor_reduce(ext2[0:G, 1:2], bank[1][0:G, 0:P], AX.X, ALU.max).then_inc(ext2_ready, 1)
            dve.wait_ge(ext2_ready, 2)
            dve.tensor_tensor(ext2[0:G, 2:3], ext2[0:G, 1:2], ext2[0:G, 0:1], ALU.subtract).then_inc(span_ready, 1)
            dve.wait_ge(span_ready, 1)
            dve.tensor_copy(ext_wide[0:G, 0, :], ext2[0:G, 0:1].to_broadcast([G, P])).then_inc(wide_ready, 1)
            dve.tensor_copy(ext_wide[0:G, 1, :], ext2[0:G, 2:3].to_broadcast([G, P])).then_inc(wide_ready, 1)
            dve.wait_ge(plan_wide, 2)
            dve.tensor_copy(base_row[0:1, 0:G], bank[2][0:1, 0:G]).then_inc(plan_ready, 1)
            dve.tensor_reduce(span_f[0:1, 0:1], bank[3][0:1, 0:G], AX.X, ALU.max).then_inc(widest_ready, 1)
            dve.wait_ge(widest_ready, 1)
            dve.tensor_copy(span_i[0:1, 0:1], span_f[0:1, 0:1]).then_inc(plan_ready, 1)
            dve.wait_ge(iota_set, 1)
            dve.tensor_copy(iota[:, :], iota_i).then_inc(iota_ready, 1)
            dve.wait_ge(iota_ready, 1)
            dve.wait_ge(comp_turned, 1)
            dve.wait_ge(plan_ready, 2)
            widest = dve.value_load(span_i[0:1, 0:1], min_val=0, max_val=N)
            dve.wait_ge(sums_zero, KB + C)

            def base_of(g):
                at = base_row[0:1, g:g + 1] if static(g) else base_row[0:1, bass.ds(g, 1)]
                return dve.value_load(at, min_val=0, max_val=NPAD - WIN)

            def make_hot(slot, g, base, ready):
                shape = [P, GROUP, WIN]
                return dve.tensor_tensor(
                    hot[:, slot, :, :],
                    dst_f[:, bass.ds(g * GROUP, GROUP)].rearrange("p (j o) -> p j o", o=1).to_broadcast(shape),
                    iota[:, bass.ds(base, WIN)].rearrange("p (o w) -> p o w", o=1).to_broadcast(shape),
                    ALU.is_equal).then_inc(ready, 1)

            def layer0(windows):
                def comp_of_edges(q, g):
                    dve.tensor_tensor(
                        type_hot[:, :, :],
                        typ_f[:, bass.ds(g * GROUP, GROUP)].rearrange("p (j o) -> p j o", o=1).to_broadcast([P, GROUP, NR]),
                        iota[:, 0:NR].rearrange("p (o r) -> p o r", o=1).to_broadcast([P, GROUP, NR]),
                        ALU.is_equal).then_inc(type_hot_ready, 1)
                    dve.wait_ge(type_hot_ready, g + 1)
                    shape = [P, GROUP, NB, NR]
                    dve.tensor_tensor(
                        comp_prod[:, :, :, :],
                        type_hot[:, :, :].rearrange("p j (o r) -> p j o r", o=1).to_broadcast(shape),
                        comp_T[:, :, :].rearrange("p (o b) r -> p o b r", o=1).to_broadcast(shape),
                        ALU.mult).then_inc(comp_prod_ready, 1)
                    dve.wait_ge(comp_prod_ready, g + 1)
                    dve.tensor_reduce(comp_e[:, q, :, :], comp_prod[:, :, :, :], AX.X, ALU.add).then_inc(comp_e_ready, 1)
                    dve.wait_ge(comp_e_ready, g + 1)

                def weigh(q, slot, g, s, base, first):
                    make_hot(slot, g, base, hot0_ready)
                    dve.wait_ge(hot0_ready, s + 1)
                    if not first:
                        dve.wait_ge(sum0_ready, s - 1)
                    shape = [P, GROUP, NB, WIN]
                    dve.tensor_tensor(
                        whot[:, slot, :, :, :],
                        hot[:, slot, :, :].rearrange("p j (o w) -> p j o w", o=1).to_broadcast(shape),
                        comp_e[:, q, :, :].rearrange("p j (b o) -> p j b o", o=1).to_broadcast(shape),
                        ALU.mult).then_inc(whot_ready, 1)

                def add(slot, s, base):
                    dve.wait_ge(sum0_ready, s + 1)
                    if not (static(s) and s == 0):
                        dve.wait_ge(sum0_added, s)
                    to = sumT0[:, :, bass.ds(base, WIN)]
                    dve.tensor_tensor(to, to, bank[6 + slot][:, 0:KB * WIN].rearrange("p (k w) -> p k w", k=KB),
                                      ALU.add).then_inc(sum0_added, 1)

                def release_rows():
                    dve.sem_inc(x_used, 1)

                if windows == 1:
                    def group(q, g, i):
                        comp_of_edges(q, g)
                        weigh(q, q, g, g, base_of(g), static(g) and g < 2)
                        if not (static(g) and g == 0):
                            add(1 - q, g - 1, base_of(g - 1))
                            release_rows()

                    pairs(dve, group)
                    add(0, G - 1, base_of(G - 1))
                    release_rows()
                else:
                    def group(q, g, i):
                        comp_of_edges(q, g)
                        settle(dve)
                        first = static(g) and g == 0
                        if first:
                            for w in range(2):
                                weigh(q, w, g, w, w * WIN, True)
                                add(w, w, w * WIN)
                        with dve.Fori(1 if first else 0, windows // 2) as w:
                            for v in range(2):
                                s = g * windows + 2 * w + v
                                weigh(q, v, g, s, (2 * w + v) * WIN, False)
                                add(v, s, (2 * w + v) * WIN)
                        release_rows()

                    pairs(dve, group)
                dve.wait_ge(sum0_added, G * windows)
                dve.sem_inc(layer0_summed, 1)

            with dve.If(widest < WIN):
                layer0(1)
            with dve.Else():
                layer0(NWIN)

            dve.wait_ge(weights_in, 16 * 15)
            dve.wait_ge(b2_in, 32)
            dve.tensor_copy(we_hi[:, :], we[:, :]).then_inc(w_hi, 1)
            dve.tensor_copy(w2_hi[:, :, :], w2[:, :, :]).then_inc(w_hi, 1)
            dve.tensor_copy(b2_r[:, :], b2_two[:, :]).then_inc(w_hi, 1)
            dve.wait_ge(w_hi, 3)
            dve.tensor_tensor(we_lo[:, :], we[:, :], we_hi[:, :].bitcast(F32), ALU.subtract).then_inc(split_w, 2)
            dve.tensor_tensor(w2_lo[:, :, :], w2[:, :, :], w2_hi[:, :, :].bitcast(F32), ALU.subtract).then_inc(split_w, 2)
            dve.tensor_tensor(b2_r[32:33, :], b2_two[32:33, :], b2_r[32:33, :].bitcast(F32),
                              ALU.subtract).then_inc(split_w, 2)

            T = NODE_TILE

            def variance(q, n, of, stats_sem, var_sem, s):
                dve.bn_stats(stats[0:T, q, :], of).then_inc(stats_sem, 1)
                dve.wait_ge(stats_sem, s + 1)
                settle(dve)
                dve.bn_aggr(mv[0:T, q, :], stats[0:T, q, :]).then_inc(var_sem, 1)

            def norm(q, to, of, std_sem, rstd_sem, norm_sem, s):
                dve.wait_ge(std_sem, s + 1)
                dve.reciprocal(rstd[0:T, q, :], std[0:T, q, :]).then_inc(rstd_sem, 1)
                dve.wait_ge(rstd_sem, s + 1)
                dve.tensor_scalar(to, of, mv[0:T, q, 0:1], rstd[0:T, q, 0:1], ALU.subtract,
                                  ALU.mult).then_inc(norm_sem, 1)

            def mixed_rows(q, n, i):
                dve.wait_ge(mixed, n + 1)
                dve.wait_ge(node_in[q], 32 * (i + 1))
                dve.tensor_tensor(y[0:T, q, :], bank[q][0:T, 0:D], x_s[0:T, q, :], ALU.add).then_inc(mix_used, 1)
                dve.wait_ge(mix_used, n + 1)
                dve.tensor_tensor(y2[0:T, q, :], y[0:T, q, :], bias0_bc[0:T, :], ALU.add).then_inc(y_ready, 1)
                dve.wait_ge(y_ready, n + 1)
                variance(q, n, y2[0:T, q, :], stats_ready, var_ready, n)

            def node_tile(q, n, i):
                if not (static(n) and n < 2):
                    dve.wait_ge(x1_out[q], 16 * i)
                    dve.wait_ge(x1_turned, n - 1)
                norm(q, x1_s[0:T, q, :], y2[0:T, q, :], std_ready, rstd_ready, x1_ready, n)
                if not (static(n) and n >= NT - 1):
                    mixed_rows(1 - q, n + 1, i + q)
                dve.wait_ge(table_mm, n + 1)
                if not (static(n) and n < 2):
                    dve.wait_ge(table_out[q], 16 * i)
                dve.tensor_tensor(table_s[0:T, q, :], bank[4 + q][0:T, :], bx_bc[0:T, :], ALU.add).then_inc(table_ready, 1)

            mixed_rows(0, 0, 0)
            node_pairs(dve, node_tile)

            def split_lo(g, q):
                dve.wait_ge(edge_hi, g + 1)
                dve.tensor_tensor(edge_r[DE:P, q, :], edge_f[DE:P, q, :], edge_r[DE:P, q, :].bitcast(F32),
                                  ALU.subtract).then_inc(edge_split, 1)

            def layer1(windows):
                split_lo(0, 0)

                def hot1(slot, g, s, base, first):
                    if not first:
                        dve.wait_ge(sum1_ready, s - 1)
                    make_hot(slot, g, base, hot1_ready)

                def add(slot, s, base):
                    dve.wait_ge(sum1_ready, s + 1)
                    if not (static(s) and s == 0):
                        dve.wait_ge(sum1_added, s)
                    to = sumT1[:, :, bass.ds(base, WIN)]
                    dve.tensor_tensor(to, to, bank[6 + slot][:, 0:C * WIN].rearrange("p (c w) -> p c w", c=C),
                                      ALU.add).then_inc(sum1_added, 1)

                def tick(k, i):
                    if at := group_at(k, i, -2):
                        split_lo(*at)
                    if at := tile_at(k, i, 0):
                        t, ten, two = at
                        if at := group_at(k, i, 0):
                            dve.wait_ge(row_in[at[1]], 16 * GROUP * (i + 1))
                        dve.wait_ge(z_ready, t + 1)
                        dve.tensor_tensor(rows[:, ten, :], bank[two][:, :], rows[:, ten, :], ALU.add).then_inc(pre_ready, 1)
                    if at := tile_at(k, i, 1):
                        t, ten, two = at
                        dve.wait_ge(hi_ready, t + 1)
                        dve.scalar_tensor_tensor(out=h_lo[:, two, :], in0=bank[2 + two][:, 0:D], scalar=0.0,
                                                 in1=h_hi[:, two, :].bitcast(F32), op0=ALU.max,
                                                 op1=ALU.subtract).then_inc(lo_ready, 1)
                    if at := tile_at(k, i, 2):
                        t, ten, two = at
                        if (at := group_at(k, i, 2)) and not (static(at[0]) and at[0] < 2):
                            dve.wait_ge(sum1_ready, (at[0] - 1) * windows)
                        dve.wait_ge(gate_ready, t + 1)
                        dve.wait_ge(core_ready, t + 1)
                        dve.tensor_tensor(msg[:, ten, :], rows[:, ten, D:2 * D], bank[4 + two][:, 0:D],
                                          ALU.mult).then_inc(msg_ready, 1)
                    if windows == 1:
                        if at := group_at(k, i, 7):
                            g, q = at
                            hot1(q, g, g, base_of(g), static(g) and g < 2)
                        if at := group_at(k, i, 9):
                            g, q = at
                            add(q, g, base_of(g))
                    elif at := group_at(k, i, 8):
                        g, q = at
                        first = static(g) and g == 0
                        if first:
                            for w in range(2):
                                hot1(w, g, w, w * WIN, True)
                                add(w, w, w * WIN)
                        with dve.Fori(1 if first else 0, windows // 2) as w:
                            for v in range(2):
                                s = g * windows + 2 * w + v
                                hot1(v, g, s, (2 * w + v) * WIN, False)
                                add(v, s, (2 * w + v) * WIN)

                ticks(dve, tick)
                dve.wait_ge(sum1_added, G * windows)
                dve.sem_inc(layer1_summed, 1)

            with dve.If(widest < WIN):
                layer1(1)
            with dve.Else():
                layer1(NWIN)

            def out_tile(q, n, i):
                dve.wait_ge(sum_turned, n + 1)
                dve.wait_ge(x1_in[q], 16 * (i + 1))
                dve.tensor_tensor(y[0:T, q, :], bank[2 + q][0:T, 0:D], x_s[0:T, q, :], ALU.add).then_inc(f_sum, 1)
                dve.wait_ge(f_sum, n + 1)
                variance(q, n, y[0:T, q, :], f_stats, f_var, 2 * n)
                norm(q, y2[0:T, q, :], y[0:T, q, :], f_std, f_rstd, f_norm, 2 * n)
                dve.wait_ge(f_norm, 2 * n + 1)
                dve.tensor_tensor(y[0:T, q, :], y2[0:T, q, :], gamma_bc[0:T, :], ALU.mult).then_inc(f_scaled, 1)
                dve.wait_ge(f_scaled, n + 1)
                dve.tensor_tensor(y2[0:T, q, :], y[0:T, q, :], beta_bc[0:T, :], ALU.add).then_inc(f_shifted, 1)
                dve.wait_ge(f_shifted, n + 1)
                dve.tensor_tensor(y[0:T, q, :], y2[0:T, q, :], x_s[0:T, q, :], ALU.add).then_inc(f_res, 1)
                dve.wait_ge(f_res, n + 1)
                variance(q, n, y[0:T, q, :], f_stats, f_var, 2 * n + 1)
                if not (static(n) and n < 2):
                    dve.wait_ge(out_done[q], 16 * i)
                norm(q, x1_s[0:T, q, :], y[0:T, q, :], f_std, f_rstd, f_norm, 2 * n + 1)
                dve.wait_ge(f_norm, 2 * n + 2)
                dve.sem_inc(out_ready, 1)

            for q in range(2):
                dve.wait_ge(x1_out[q], 16 * (NT // 2))
            node_pairs(dve, out_tile)


def kernel(x, src, dst, edge_attr_64, edge_type_8, L0_gnn_basis, L0_gnn_comp, L0_gnn_loop_weight,
           L0_gnn_bias_param, L1_gnn_W1, L1_gnn_b1, L1_gnn_W2, L1_gnn_b2, L1_gnn_Wg, L1_gnn_bg,
           L1_gnn_gamma, L1_gnn_beta):
    import numpy as np
    import concourse.bacc as bacc
    from concourse.bass_utils import run_bass_kernel_spmd

    x = np.asarray(x)
    N, D = x.shape
    E = np.asarray(src).shape[0]
    tiles = E // P

    def laid(a):
        return np.ascontiguousarray(np.asarray(a))

    arrays = {
        "x": laid(x),
        "xT": laid(x.T.reshape(D // P, P, N).transpose(1, 0, 2)),
        "src": laid(np.asarray(src).reshape(tiles // GROUP, GROUP, P).transpose(0, 2, 1)),
        "dst": laid(np.asarray(dst).reshape(tiles, P).T),
        "etype": laid(np.asarray(edge_type_8).reshape(tiles, P).T),
        "edge_T": laid(np.asarray(edge_attr_64).T),
        "basis": laid(L0_gnn_basis), "comp": laid(L0_gnn_comp), "loop_w": laid(L0_gnn_loop_weight),
        "bias0": laid(L0_gnn_bias_param), "W1": laid(L1_gnn_W1), "b1": laid(L1_gnn_b1), "W2": laid(L1_gnn_W2),
        "b2": laid(L1_gnn_b2), "Wg": laid(L1_gnn_Wg), "bg": laid(L1_gnn_bg), "gamma": laid(L1_gnn_gamma),
        "beta": laid(L1_gnn_beta),
    }
    nc = bacc.Bacc("TRN2", target_bir_lowering=False, num_devices=1)
    args = {name: nc.dram_tensor(f"in_{name}", a.shape, mybir.dt.from_np(a.dtype), kind="ExternalInput").ap()
            for name, a in arrays.items()}
    out = nc.dram_tensor("out_rows", [N, D], F32, kind="ExternalOutput").ap()
    build(nc, **args, out=out)
    r = run_bass_kernel_spmd(nc, [{f"in_{name}": a for name, a in arrays.items()}], core_ids=[0])
    return r.results[0]["out_rows"]
```

```python
from contextlib import ExitStack

import concourse.bass as bass
from concourse import mybir

F32 = mybir.dt.float32
F32R = mybir.dt.float32r
I32 = mybir.dt.int32
ALU = mybir.AluOpType
ACT = mybir.ActivationFunctionType
AX = mybir.AxisListType

P = 128
GROUP = 5
RING0 = 4
RING_F = 4
WIN = 32
NODE_TILE = 125
EPS = 1e-5


def build(nc, x, xT, src, dst, etype, edge_T, basis, comp, loop_w, bias0,
          W1, b1, W2, b2, Wg, bg, gamma, beta, out):
    N, D = x.shape
    G = src.shape[0]
    TILES = G * GROUP
    DE = edge_T.shape[0]
    NB, NR = basis.shape[0], comp.shape[0]
    C = D // P
    NT = N // NODE_TILE
    PAIRS = G // 2
    NWIN = 2 * -(-N // (2 * WIN))
    NPAD = NWIN * WIN
    KB = C * NB
    assert G % 2 == 1 and NT * NODE_TILE == N and NT % RING_F == 0 and NT < G // RING0 and 2 * DE == P and KB == 8
    GE = GROUP * P

    h_table = nc.dram_tensor("node_table", [N, 2 * D], F32, kind="Internal").ap()
    x1_dram = nc.dram_tensor("x1_rows", [N, D], F32, kind="Internal").ap()

    ctx = ExitStack()
    with ctx:
        def sb(name, shape, dt=F32):
            return ctx.enter_context(nc.sbuf_tensor(name, shape, dt))

        def sem(name):
            return ctx.enter_context(nc.semaphore(name))

        bank = [ctx.enter_context(nc.psum_tensor(f"bank{i}", [P, 512], F32)) for i in range(8)]

        ident = sb("ident", [P, P])
        iota = sb("iota", [P, NPAD])
        ones_r = sb("ones_r", [64, P], F32R)
        zero = sb("zero", [P, 1])
        dst_f = sb("dst_f", [P, TILES])
        typ_f = sb("typ_f", [P, TILES])
        dst_rel = sb("dst_rel", [P, TILES])
        src_slot = sb("src_slot", [P, RING0, GROUP], I32)
        ext = sb("ext", [P, 2, P])
        ext2 = sb("ext2", [P, 4])
        ext_wide = sb("ext_wide", [P, 2, P])
        base_row = sb("base_row", [1, P], I32)
        span_f = sb("span_f", [1, 2])
        span_i = sb("span_i", [1, 2], I32)
        basis_sb = sb("basis_sb", [P, KB, D])
        loop_sb = sb("loop_sb", [P, C, D])
        comp_bc = sb("comp_bc", [P, NR * NB])
        comp_T = sb("comp_T", [P, NB, NR])
        bias0_row = sb("bias0_row", [1, D])
        ones_f = sb("ones_f", [1, P])
        wx = sb("wx", [P, C, 2 * D])
        bx_bc = sb("bx_bc", [P, 2 * D])
        we = sb("we", [P, 2 * D])
        we_hi = sb("we_hi", [P, 2 * D], F32R)
        we_lo = sb("we_lo", [P, 2 * D], F32R)
        w2 = sb("w2", [P, C, D])
        w2_hi = sb("w2_hi", [P, C, D], F32R)
        w2_lo = sb("w2_lo", [P, C, D], F32R)
        b2_two = sb("b2_two", [64, D])
        b2_r = sb("b2_r", [64, D], F32R)
        gamma_bc = sb("gamma_bc", [P, D])
        beta_bc = sb("beta_bc", [P, D])
        rows = sb("rows", [P, 2 * GROUP, 2 * D])
        sumT1 = sb("sumT1", [P, C, NPAD])
        hot = sb("hot", [P, 2, GROUP, WIN])
        hot_r = sb("hot_r", [P, 2, GROUP, WIN], F32R)

        xT_s = sb("xT_s", [P, C, NODE_TILE])
        stats = sb("stats", [P, 2, 6])
        mv = sb("mv", [P, 2, 2])
        std = sb("std", [P, 2, 1])
        rstd = sb("rstd", [P, 2, 1])
        eps = sb("eps", [P, 1])

        ctx0 = ExitStack()
        with ctx0:
            def sb0(name, shape, dt=F32):
                return ctx0.enter_context(nc.sbuf_tensor(name, shape, dt))

            sumT0 = sb0("sumT0", [P, KB, NPAD])
            with ExitStack() as ctx_i:
                iota_i = ctx_i.enter_context(nc.sbuf_tensor("iota_i", [P, NPAD], I32))
                dst_i = ctx_i.enter_context(nc.sbuf_tensor("dst_i", [P, TILES], I32))
                typ_i = ctx_i.enter_context(nc.sbuf_tensor("typ_i", [P, TILES], I32))
            root = sb0("root", [P, NT, D])
            type_hot = sb0("type_hot", [P, GROUP, NR])
            comp_prod = sb0("comp_prod", [P, GROUP, NB, NR])
            comp_e = sb0("comp_e", [P, 2, GROUP, NB])
            whot = sb0("whot", [P, 2, GROUP, NB, WIN])
        edge_f = sb("edge_f", [P, 2, GE])
        edge_r = sb("edge_r", [P, 2, GE], F32R)
        h_hi = sb("h_hi", [P, GROUP, D], F32R)
        h_lo = sb("h_lo", [P, GROUP, D], F32R)
        msg = sb("msg", [P, GROUP, D])
        msg_hi = sb("msg_hi", [P, 2 * GROUP, D], F32R)
        msg_lo = sb("msg_lo", [P, 2 * GROUP, D], F32R)
        sum_rows = sb("sum_rows", [WIN, D])
        f_x, f_xb, f_y, f_w, f_z, f_r, f_o = (
            sb(f"f_{s}", [P, RING_F, D]) for s in ("x", "xb", "y", "w", "z", "r", "o"))
        f_stats = sb("f_stats", [P, 2, RING_F, 6])
        f_mv = sb("f_mv", [P, 2, RING_F, 2])
        f_std = sb("f_std", [P, 2, RING_F])
        f_rstd = sb("f_rstd", [P, 2, RING_F])
        f_shift = sb("f_shift", [P, 2, RING_F])
        rows_flat = rows[:, :, :].rearrange("p t n -> p (t n)")
        cuts = [0]

        def cut(*shape):
            size = 1
            for n in shape:
                size *= n
            cuts.append(cuts[-1] + size)
            assert cuts[-1] <= 4 * GROUP * D
            return rows_flat[:, cuts[-2]:cuts[-1]]

        stage = cut(2, KB, NODE_TILE).rearrange("p (q k n) -> p q k n", q=2, k=KB)
        table_s = cut(2, 2 * D).rearrange("p (q n) -> p q n", q=2)
        y = cut(2, D).rearrange("p (q n) -> p q n", q=2)
        x1_s = cut(2, D).rearrange("p (q n) -> p q n", q=2)
        x1T = cut(2, C, NODE_TILE).rearrange("p (q c n) -> p q c n", q=2, c=C)

        ident_set, iota_set, consts = sem("ident_set"), sem("iota_set"), sem("consts")
        edges_in, weights_in, b2_in = sem("edges_in"), sem("weights_in"), sem("b2_in")
        pool_zeroed, floats_ready, iota_ready, rel_ready = (
            sem("pool_zeroed"), sem("floats_ready"), sem("iota_ready"), sem("rel_ready"))
        ext_ready, ext_turned, ext2_ready, span_ready, wide_ready, plan_wide, widest_ready, plan_ready = (
            sem("ext_ready"), sem("ext_turned"), sem("ext2_ready"), sem("span_ready"), sem("wide_ready"),
            sem("plan_wide"), sem("widest_ready"), sem("plan_ready"))
        sums_zero, comp_turned, split_w, w_hi = sem("sums_zero"), sem("comp_turned"), sem("split_w"), sem("w_hi")
        src0_in = [sem(f"src0_in{q}") for q in range(RING0)]
        x_in = [sem(f"x_in{q}") for q in range(RING0)]
        x_used = sem("x_used")
        type_hot_ready, comp_prod_ready, comp_e_ready = (
            sem("type_hot_ready"), sem("comp_prod_ready"), sem("comp_e_ready"))
        hot0_ready, whot_ready, sum0_ready, sum0_added, layer0_summed = (
            sem("hot0_ready"), sem("whot_ready"), sem("sum0_ready"), sem("sum0_added"), sem("layer0_summed"))
        xT_in, root_mm, root_kept = sem("xT_in"), sem("root_mm"), sem("root_kept")
        staged, mixed, y_ready, stats_ready, var_ready, std_ready, rstd_ready = (
            sem("staged"), sem("mixed"), sem("y_ready"), sem("stats_ready"), sem("var_ready"),
            sem("std_ready"), sem("rstd_ready"))
        x1_ready, x1_turned, x1T_ready = sem("x1_ready"), sem("x1_turned"), sem("x1T_ready")
        table_mm, table_ready = sem("table_mm"), sem("table_ready")
        x1_out, table_out = [sem(f"x1_out{q}") for q in range(2)], [sem(f"table_out{q}") for q in range(2)]
        src1_in = [sem(f"src1_in{q}") for q in range(2)]
        edge_in = [sem(f"edge_in{q}") for q in range(2)]
        edge_hi, edge_split = sem("edge_hi"), sem("edge_split")
        row_in = [sem(f"row_in{q}") for q in range(2 * GROUP)]
        z_ready, pre_ready, gate_ready, turned = (
            sem("z_ready"), sem("pre_ready"), sem("gate_ready"), sem("turned"))
        hi_ready, lo_ready, core_ready, msg_ready = (
            sem("hi_ready"), sem("lo_ready"), sem("core_ready"), sem("msg_ready"))
        msg_hi_ready, lo_by_pool, lo_by_dve = sem("msg_hi_ready"), sem("lo_by_pool"), sem("lo_by_dve")
        hot1_ready, sum1_ready, sum1_kept, sum1_turned, sum1_added, layer1_summed = (
            sem("hot1_ready"), sem("sum1_ready"), sem("sum1_kept"), sem("sum1_turned"), sem("sum1_added"),
            sem("layer1_summed"))
        x1_in = [sem(f"x1_in{q}") for q in range(RING_F)]
        sum_staged, sum_turned, fy_ready, fxb_ready, fz_ready, fr_ready = (
            sem(s) for s in ("sum_staged", "sum_turned", "fy_ready", "fxb_ready", "fz_ready", "fr_ready"))
        fstats_ready, fvar_ready, fstd_ready, frstd_ready, fshift_ready, fnorm_ready = (
            [sem(f"{s}{h}") for h in range(2)]
            for s in ("fstats_ready", "fvar_ready", "fstd_ready", "frstd_ready", "fshift_ready", "fnorm_ready"))
        passed = sem("passed")
        out_done = [sem(f"out_done{q}") for q in range(RING_F)]

        def static(v):
            return isinstance(v, int)

        def rounds(eng, ring, step):
            for q in range(ring):
                step(q, q, 0)
            with eng.Fori(1, G // ring) as i:
                for q in range(ring):
                    step(q, ring * i + q, i)
            for q in range(G % ring):
                step(q, G - G % ring + q, G // ring)

        def rounds_and_nodes(eng, step, node):
            for q in range(RING0):
                step(q, q, 0)
            node(0)
            step_round = G // RING0
            with eng.Fori(1, NT) as i:
                for q in range(RING0):
                    step(q, RING0 * i + q, i)
                node(i)
            with eng.Fori(NT, step_round) as i:
                for q in range(RING0):
                    step(q, RING0 * i + q, i)
            for q in range(G % RING0):
                step(q, G - G % RING0 + q, step_round)

        def node_ticks(eng, tick):
            last = NT // RING_F
            for i in range(2):
                for k in range(RING_F):
                    tick(k, i)
            with eng.Fori(2, last - 1) as i:
                for k in range(RING_F):
                    tick(k, i)
            for i in (last - 1, last):
                for k in range(RING_F):
                    tick(k, i)

        def node_at(k, i, lag):
            if static(i) and not 0 <= RING_F * i + k - lag < NT:
                return None
            return RING_F * i + (k - lag), (k - lag) % RING_F

        def node_pairs(eng, step):
            step(0, 0, 0)
            step(1, 1, 0)
            with eng.Fori(1, NT // 2 - 1) as i:
                step(0, 2 * i, i)
                step(1, 2 * i + 1, i)
            step(0, NT - 2, NT // 2 - 1)
            step(1, NT - 1, NT // 2 - 1)

        def ticks(eng, tick):
            for i in range(2):
                for k in range(2 * GROUP):
                    tick(k, i)
            with eng.Fori(2, PAIRS) as i:
                for k in range(2 * GROUP):
                    tick(k, i)
            for k in range(3 * GROUP + 1):
                tick(k, PAIRS)

        def tile_at(k, i, lag):
            if static(i) and not 0 <= 2 * GROUP * i + k - lag < TILES:
                return None
            return 2 * GROUP * i + (k - lag), (k - lag) % (2 * GROUP), (k - lag) % GROUP, (k - lag) % 2

        def group_at(k, i, lag):
            at = tile_at(k, i, lag)
            if at is None or (k - lag) % GROUP:
                return None
            return 2 * i + (k - lag) // GROUP, ((k - lag) // GROUP) % 2

        def settle(eng):
            eng.sem_inc(passed, 1)

        def nodes(n):
            return bass.ds(n * NODE_TILE, NODE_TILE)

        block = ctx.enter_context(nc.Block())

        @block.sync
        def _(sp):
            sp.dma_start(dst_i[:, :], dst).then_inc(edges_in, 16)
            sp.dma_start(typ_i[:, :], etype).then_inc(edges_in, 16)
            sp.dma_start(comp_bc[:, :],
                         comp.rearrange("(o r) b -> o (r b)", o=1).to_broadcast([P, NR * NB])).then_inc(edges_in, 16)

            def load_src0(q, g, i):
                if not (static(g) and g < RING0):
                    sp.wait_ge(x_in[q], 16 * GROUP * i)
                sp.dma_start(src_slot[:, q, :], src[g, :, :]).then_inc(src0_in[q], 16)

            rounds(sp, RING0, load_src0)

            def node_tile(q, n, i):
                sp.wait_ge(x1_ready, n + 1)
                sp.dma_start(x1_dram[nodes(n), :], x1_s[0:NODE_TILE, q, :]).then_inc(x1_out[q], 16)
                sp.wait_ge(table_ready, n + 1)
                sp.dma_start(h_table[nodes(n), :], table_s[0:NODE_TILE, q, :]).then_inc(table_out[q], 16)

            node_pairs(sp, node_tile)

            def load_edges(q, g, i):
                if not (static(g) and g < 2):
                    for j in range(GROUP):
                        sp.wait_ge(row_in[q * GROUP + j], 16 * i)
                sp.dma_start(src_slot[:, q, :], src[g, :, :]).then_inc(src1_in[q], 16)
                if not (static(g) and g < 2):
                    sp.wait_ge(edge_split, 2 * (g - 1))
                for half in range(2):
                    sp.dma_start(edge_f[half * DE:(half + 1) * DE, q, :],
                                 edge_T[:, bass.ds(g * GE, GE)]).then_inc(edge_in[q], 16)

            rounds(sp, 2, load_edges)

            for q in range(2):
                sp.wait_ge(x1_out[q], 16 * (NT // 2))

            def load_x1(q, n):
                sp.dma_start(f_x[0:NODE_TILE, q, :], x1_dram[nodes(n), :]).then_inc(x1_in[q], 16)

            for n in range(RING_F):
                load_x1(n, n)

            def tick(k, i):
                if at := node_at(k, i, 0):
                    n, q = at
                    if not (static(n) and n >= NT - RING_F):
                        sp.wait_ge(fy_ready, n + 1)
                        sp.wait_ge(fxb_ready, n + 1)
                        load_x1(q, n + RING_F)
                if at := node_at(k, i, 3):
                    n, q = at
                    sp.wait_ge(fnorm_ready[1], n + 1)
                    sp.dma_start(out[nodes(n), :], f_o[0:NODE_TILE, q, :]).then_inc(out_done[q], 16)

            node_ticks(sp, tick)
            for q in range(RING_F):
                sp.wait_ge(out_done[q], 16 * (NT // RING_F))

        @block.gpsimd
        def _(pool):
            pool.memset(ident[:, :], 0.0).then_inc(pool_zeroed, 1)
            pool.iota(iota_i[:, :], [[1, NPAD]], base=0, channel_multiplier=0).then_inc(iota_set, 1)
            pool.wait_ge(pool_zeroed, 1)
            pool.affine_select(out=ident[:, :], in_=ident[:, :], compare_op=ALU.not_equal, fill=1.0,
                               base=0, pattern=[[-1, P]], channel_multiplier=1).then_inc(ident_set, 1)

            x_slots = rows[:, :, :].rearrange("p t (h n) -> p (t h) n", h=2)

            def gather_x(q, g, i):
                pool.wait_ge(src0_in[q], 16 * (i + 1))
                if not (static(g) and g < RING0):
                    pool.wait_ge(x_used, g - (RING0 - 1))
                    settle(pool)
                for j in range(GROUP):
                    pool.indirect_dma_start(
                        out=x_slots[:, q * GROUP + j, :], out_offset=None, in_=x,
                        in_offset=bass.IndirectOffsetOnAxis(ap=src_slot[:, q, j:j + 1], axis=0)).then_inc(x_in[q], 16)

            rounds(pool, RING0, gather_x)

            for q in range(2):
                pool.wait_ge(table_out[q], 16 * (NT // 2))
                pool.wait_ge(x1_out[q], 16 * (NT // 2))

            def gather_row(k, i, lag):
                t, ten, five, _ = tile_at(k, i, lag)
                if at := group_at(k, i, lag):
                    pool.wait_ge(src1_in[at[1]], 16 * (i + (k - lag) // (2 * GROUP) + 1))
                    settle(pool)
                if not (static(t) and t < 2 * GROUP):
                    pool.wait_ge(msg_ready, t - (2 * GROUP - 1))
                    settle(pool)
                pool.indirect_dma_start(
                    out=rows[:, ten, :], out_offset=None, in_=h_table,
                    in_offset=bass.IndirectOffsetOnAxis(ap=src_slot[:, ten // GROUP, five:five + 1], axis=0)
                ).then_inc(row_in[ten], 16)

            def tick(k, i):
                if tile_at(k, i, -GROUP):
                    gather_row(k, i, -GROUP)
                at = tile_at(k, i, 6)
                if at and at[2] % 2 == 0:
                    t, ten, five, _ = at
                    pool.wait_ge(msg_hi_ready, t + 1)
                    pool.tensor_tensor(msg_lo[:, ten, :], msg[:, five, :], msg_hi[:, ten, :].bitcast(F32),
                                       ALU.subtract).then_inc(lo_by_pool, 1)

            for t in range(GROUP):
                gather_row(t, 0, 0)
            ticks(pool, tick)

            def node_tick(k, i):
                if at := node_at(k, i, 0):
                    n, q = at
                    pool.wait_ge(x1_in[q], 16 * (i + 1))
                    if not (static(n) and n < RING_F):
                        pool.wait_ge(fr_ready, n - (RING_F - 1))
                    settle(pool)
                    pool.tensor_tensor(f_xb[0:NODE_TILE, q, :], f_x[0:NODE_TILE, q, :], beta_bc[0:NODE_TILE, :],
                                       ALU.add).then_inc(fxb_ready, 1)

            pool.wait_ge(weights_in, 16 * 16)
            node_ticks(pool, node_tick)

        @block.scalar
        def _(act):
            def row(v, n):
                return v.rearrange("(o n) -> o n", o=1).to_broadcast([P, n])

            act.wait_ge(consts, 5)
            for k in range(2, KB):
                act.activation(sumT0[:, k, :], zero[:, 0:1].to_broadcast([P, NPAD]), ACT.Copy).then_inc(sums_zero, 1)
            b2_row = b2.rearrange("(o n) -> o n", o=1)
            for to, at in [
                (loop_sb[:, :, :], loop_w.rearrange("(c p) n -> p c n", p=P)),
                (bias0_row[:, :], bias0.rearrange("(o n) -> o n", o=1)),
                (basis_sb[:, 0:NB, :], basis[:, 0:P, :].rearrange("b p n -> p b n")),
                (basis_sb[:, NB:KB, :], basis[:, P:D, :].rearrange("b p n -> p b n")),
                (wx[:, :, 0:D], W1[0:D, :].rearrange("(c p) n -> p c n", p=P)),
                (wx[:, :, D:2 * D], Wg[0:D, :].rearrange("(c p) n -> p c n", p=P)),
                (bx_bc[:, 0:D], row(b1, D)),
                (bx_bc[:, D:2 * D], row(bg, D)),
                (we[0:DE, 0:D], W1[D:D + DE, :]),
                (we[DE:P, 0:D], W1[D:D + DE, :]),
                (we[0:DE, D:2 * D], Wg[D:D + DE, :]),
                (we[DE:P, D:2 * D], Wg[D:D + DE, :]),
                (w2[:, :, :], W2.rearrange("(c p) n -> p c n", p=P)),
                (gamma_bc[:, :], row(gamma, D)),
                (beta_bc[:, :], row(beta, D)),
                (b2_two[0:1, :], b2_row),
            ]:
                act.dma_start(to, at).then_inc(weights_in, 16)
            act.dma_start(b2_two[32:33, :], b2_row).then_inc(b2_in, 16)
            for c in range(C):
                act.activation(sumT1[:, c, :], zero[:, 0:1].to_broadcast([P, NPAD]), ACT.Copy).then_inc(sums_zero, 1)

            act.wait_ge(iota_ready, 1)
            act.wait_ge(floats_ready, 2)
            act.dma_start(xT_s[:, :, :], xT[:, :, nodes(0)]).then_inc(xT_in, 16)

            def keep_root(n):
                act.wait_ge(root_mm, n + 1)
                act.activation(root[0:NODE_TILE, n, :] if static(n) else
                               root[0:NODE_TILE, bass.ds(n, 1), :].rearrange("p o n -> p (o n)"),
                               bank[0][0:NODE_TILE, 0:D], ACT.Copy).then_inc(root_kept, 1)

            def next_xT(n):
                act.dma_start(xT_s[:, :, :], xT[:, :, nodes(n + 1)]).then_inc(xT_in, 16)

            with act.Fori(0, NT - 1) as n:
                keep_root(n)
                next_xT(n)
            keep_root(NT - 1)

            act.wait_ge(layer0_summed, 1)

            def stage_sums(q, n):
                act.activation(stage[:, q, :, :], sumT0[:, :, nodes(n)], ACT.Copy).then_inc(staged, 1)

            def node_tile(q, n, i):
                act.wait_ge(var_ready, n + 1)
                act.activation(std[0:NODE_TILE, q, :], mv[0:NODE_TILE, q, 1:2], ACT.Sqrt,
                               bias=eps[0:NODE_TILE, 0:1]).then_inc(std_ready, 1)
                act.wait_ge(mixed, n + 1)
                if not (static(n) and n >= NT - 2):
                    stage_sums(q, n + 2)
                act.wait_ge(x1_turned, n + 1)
                if not (static(n) and n < 2):
                    act.wait_ge(table_mm, n - 1)
                act.activation(x1T[:, q, :, :].rearrange("p c n -> p (c n)"), bank[2 + q][:, 0:C * NODE_TILE],
                               ACT.Copy).then_inc(x1T_ready, 1)

            stage_sums(0, 0)
            stage_sums(1, 1)
            node_pairs(act, node_tile)

            def split_hi(g, q, i):
                act.wait_ge(edge_in[q], 32 * (i + 1))
                if not (static(g) and g < 2):
                    act.wait_ge(z_ready, GROUP * (g - 1))
                act.activation(edge_r[:, q, :], edge_f[:, q, :], ACT.Copy).then_inc(edge_hi, 1)

            split_hi(0, 0, 0)
            split_hi(1, 1, 0)
            widest = act.value_load(span_i[0:1, 0:1], min_val=0, max_val=N)

            def layer1(windows):
                def keep(s):
                    act.wait_ge(sum1_ready, s + 1)
                    if not (static(s) and s == 0):
                        act.wait_ge(sum1_turned, s)
                    act.activation(sum_rows[:, :], bank[6][0:WIN, 0:D], ACT.Copy).then_inc(sum1_kept, 1)

                def tick(k, i):
                    at = group_at(k, i, -GROUP)
                    if at and not (static(at[0]) and at[0] < 2):
                        split_hi(*at, i + (k + GROUP) // (2 * GROUP))
                    if at := tile_at(k, i, 1):
                        t, ten, _, _ = at
                        act.wait_ge(pre_ready, t + 1)
                        act.activation(rows[:, ten, D:2 * D], rows[:, ten, D:2 * D], ACT.Sigmoid).then_inc(gate_ready, 1)
                    if at := tile_at(k, i, 5):
                        t, ten, five, _ = at
                        if (at := group_at(k, i, 5)) and not (static(at[0]) and at[0] < 2):
                            act.wait_ge(sum1_ready, (at[0] - 1) * windows)
                        act.wait_ge(msg_ready, t + 1)
                        act.activation(msg_hi[:, ten, :], msg[:, five, :], ACT.Copy).then_inc(msg_hi_ready, 1)
                    if at := tile_at(k, i, 1):
                        t, _, five, two = at
                        act.wait_ge(turned, t + 1)
                        if not (static(t) and t < GROUP):
                            act.wait_ge(core_ready, t - (GROUP - 1))
                        act.activation(h_hi[:, five, :], bank[2 + two][:, 0:D], ACT.Relu).then_inc(hi_ready, 1)
                    if windows == 1:
                        if at := group_at(k, i, 11):
                            keep(at[0])
                    elif at := group_at(k, i, 11):
                        g, q = at
                        settle(act)
                        if static(g) and g == 0:
                            keep(0)
                        with act.Fori(1 if static(g) and g == 0 else 0, windows) as w:
                            keep(g * windows + w)

                ticks(act, tick)

            with act.If(widest < WIN):
                layer1(1)
            with act.Else():
                layer1(NWIN)

            act.wait_ge(layer1_summed, 1)

            def root_of(h, n, q):
                act.wait_ge(fvar_ready[h], n + 1)
                act.activation(f_std[0:NODE_TILE, h, q:q + 1], f_mv[0:NODE_TILE, h, q, 1:2], ACT.Sqrt,
                               bias=eps[0:NODE_TILE, 0:1]).then_inc(fstd_ready[h], 1)

            def norm_of(h, n, q, to, of):
                act.wait_ge(fshift_ready[h], n + 1)
                act.activation(to[0:NODE_TILE, q, :], of[0:NODE_TILE, q, :], ACT.Identity,
                               scale=f_rstd[0:NODE_TILE, h, q:q + 1],
                               bias=f_shift[0:NODE_TILE, h, q:q + 1]).then_inc(fnorm_ready[h], 1)

            def node_tick(k, i):
                if at := node_at(k, i, -1):
                    n, q = at
                    if not (static(n) and n < 2):
                        act.wait_ge(sum_turned, n - 1)
                    act.activation(stage[:, q % 2, 0:C, :], sumT1[:, :, nodes(n)], ACT.Copy).then_inc(sum_staged, 1)
                if at := node_at(k, i, 1):
                    n, q = at
                    if not (static(n) and n < RING_F):
                        act.wait_ge(fz_ready, n - (RING_F - 1))
                    norm_of(0, n, q, f_w, f_y)
                if at := node_at(k, i, 0):
                    root_of(0, *at)
                if at := node_at(k, i, 3):
                    n, q = at
                    if not (static(n) and n < RING_F):
                        act.wait_ge(out_done[q], 16 * (i - (1 if k < 3 else 0)))
                    norm_of(1, n, q, f_o, f_r)
                if at := node_at(k, i, 2):
                    root_of(1, *at)

            act.activation(stage[:, 0, 0:C, :], sumT1[:, :, nodes(0)], ACT.Copy).then_inc(sum_staged, 1)
            node_ticks(act, node_tick)

        @block.tensor
        def _(pe):
            pe.wait_ge(ident_set, 1)
            pe.wait_ge(ext_ready, 2)
            for s in range(2):
                pe.transpose(bank[s][0:G, 0:P], ext[:, s, 0:G], ident[:, :]).then_inc(ext_turned, 1)
            pe.wait_ge(wide_ready, 2)
            for s in range(2):
                pe.matmul(bank[2 + s][:, 0:G], ext_wide[0:G, s, :], ident[0:G, 0:G]).then_inc(plan_wide, 1)
            pe.wait_ge(plan_ready, 2)
            widest = pe.value_load(span_i[0:1, 0:1], min_val=0, max_val=N)

            x_slots = rows[:, :, :].rearrange("p t (h n) -> p (t h) n", h=2)

            def root_of(n):
                pe.wait_ge(xT_in, 16 * (n + 1))
                if static(n):
                    pe.wait_ge(weights_in, 16 * 16)
                    assert n == 0
                else:
                    pe.wait_ge(root_kept, n)
                to = bank[0][0:NODE_TILE, 0:D]
                pe.matmul(to, ones_f[0:1, 0:NODE_TILE], bias0_row[0:1, :], start=True, stop=False)
                for c in range(C):
                    pe.matmul(bank[0][0:NODE_TILE, c * P:(c + 1) * P], xT_s[:, c, :], ident[:, :],
                              start=False, stop=False, skip_group_check=True)
                for c in range(C):
                    last = pe.matmul(to, xT_s[:, c, :], loop_sb[:, c, :], start=False, stop=(c == C - 1))
                last.then_inc(root_mm, 1)

            def layer0(windows):
                def step(q, slot, s, first):
                    pe.wait_ge(whot_ready, s + 1)
                    if not first:
                        pe.wait_ge(sum0_added, s - 1)
                    for c in range(C):
                        for j in range(GROUP):
                            last = pe.matmul(bank[6 + slot][:, c * NB * WIN:(c + 1) * NB * WIN],
                                             x_slots[:, q * GROUP + j, c * P:(c + 1) * P],
                                             whot[:, slot, j, :, :].rearrange("p b w -> p (b w)"),
                                             start=(j == 0), stop=(j == GROUP - 1))
                    last.then_inc(sum0_ready, 1)

                def group(q, g, i):
                    pe.wait_ge(x_in[q], 16 * GROUP * (i + 1))
                    if windows == 1:
                        step(q, q % 2, g, static(g) and g < 2)
                        return
                    first = static(g) and g == 0
                    settle(pe)
                    if first:
                        for w in range(2):
                            step(q, w, w, True)
                    with pe.Fori(1 if first else 0, windows // 2 - 1) as w:
                        for v in range(2):
                            step(q, v, g * windows + 2 * w + v, False)
                    step(q, 0, g * windows + windows - 2, False)
                    step(q, 1, g * windows + windows - 1, False)

                rounds_and_nodes(pe, group, root_of)

            with pe.If(widest < WIN):
                layer0(1)
            with pe.Else():
                layer0(NWIN)

            def mix(q, n):
                pe.wait_ge(staged, n + 1)
                if not (static(n) and n < 2):
                    pe.wait_ge(y_ready, n - 1)
                for k in range(KB):
                    last = pe.matmul(bank[q][0:NODE_TILE, 0:D], stage[:, q, k, :], basis_sb[:, k, :],
                                     start=(k == 0), stop=(k == KB - 1))
                last.then_inc(mixed, 1)

            def node_tile(q, n, i):
                if not (static(n) and n >= NT - 1):
                    mix(1 - q, n + 1)
                pe.wait_ge(x1_ready, n + 1)
                if not (static(n) and n < 2):
                    pe.wait_ge(x1T_ready, n - 1)
                for c in range(C):
                    last = pe.transpose(bank[2 + q][:, c * NODE_TILE:(c + 1) * NODE_TILE],
                                        x1_s[0:NODE_TILE, q, c * P:(c + 1) * P], ident[0:NODE_TILE, 0:NODE_TILE])
                last.then_inc(x1_turned, 1)
                pe.wait_ge(x1T_ready, n + 1)
                if not (static(n) and n < 2):
                    pe.wait_ge(table_ready, n - 1)
                for c in range(C):
                    last = pe.matmul(bank[4 + q][0:NODE_TILE, :], x1T[:, q, c, :], wx[:, c, :],
                                     start=(c == 0), stop=(c == C - 1))
                last.then_inc(table_mm, 1)

            pe.wait_ge(root_kept, NT)
            mix(0, 0)
            node_pairs(pe, node_tile)

            pe.wait_ge(split_w, 6)

            def layer1(windows):
                def sum_tile(q, slot, j):
                    for part in (msg_hi, msg_lo):
                        last = pe.matmul(bank[6][0:WIN, 0:D], hot_r[:, slot, j, :], part[:, q * GROUP + j, :],
                                         start=(j == 0 and part is msg_hi),
                                         stop=(j == GROUP - 1 and part is msg_lo))
                    if j == GROUP - 1:
                        last.then_inc(sum1_ready, 1)

                def begin(s):
                    pe.wait_ge(hot1_ready, s + 1)
                    if not (static(s) and s == 0):
                        pe.wait_ge(sum1_kept, s)

                def sums(q, slot, s):
                    begin(s)
                    for j in range(GROUP):
                        sum_tile(q, slot, j)

                def turn(s):
                    pe.wait_ge(sum1_kept, s + 1)
                    if not (static(s) and s == 0):
                        pe.wait_ge(sum1_added, s)
                    settle(pe)
                    for c in range(C):
                        last = pe.transpose(bank[7][:, c * WIN:(c + 1) * WIN], sum_rows[:, c * P:(c + 1) * P],
                                            ident[0:WIN, 0:WIN])
                    last.then_inc(sum1_turned, 1)

                def tick(k, i):
                    if at := tile_at(k, i, 0):
                        t, ten, five, two = at
                        if at := group_at(k, i, 0):
                            pe.wait_ge(edge_split, 2 * (at[0] + 1))
                        if not (static(t) and t < 2):
                            pe.wait_ge(pre_ready, t - 1)
                        lhs = edge_r[:, ten // GROUP, five * P:(five + 1) * P]
                        pe.matmul(bank[two][:, :], lhs, we_hi[:, :], start=True, stop=False)
                        pe.matmul(bank[two][:, :], lhs, we_lo[:, :], start=False, stop=True).then_inc(z_ready, 1)
                    if at := tile_at(k, i, 1):
                        t, ten, _, two = at
                        pe.wait_ge(pre_ready, t + 1)
                        if not (static(t) and t < 2):
                            pe.wait_ge(lo_ready, t - 1)
                        for c in range(C):
                            last = pe.transpose(bank[2 + two][:, c * P:(c + 1) * P],
                                                rows[:, ten, c * P:(c + 1) * P], ident[:, :])
                        last.then_inc(turned, 1)
                    if at := tile_at(k, i, 3):
                        t, _, five, two = at
                        pe.wait_ge(lo_ready, t + 1)
                        if not (static(t) and t < 2):
                            pe.wait_ge(msg_ready, t - 1)
                        to = bank[4 + two][:, 0:D]
                        pe.matmul(to, ones_r[:, :], b2_r[:, :], start=True, stop=False)
                        for c in range(C):
                            part = slice(c * P, (c + 1) * P)
                            pe.matmul(to, h_hi[:, five, part], w2_hi[:, c, :], start=False, stop=False)
                            pe.matmul(to, h_hi[:, five, part], w2_lo[:, c, :], start=False, stop=False)
                            last = pe.matmul(to, h_lo[:, five, part], w2_hi[:, c, :], start=False, stop=(c == C - 1))
                        last.then_inc(core_ready, 1)
                    at = tile_at(k, i, 7)
                    if windows == 1 and at:
                        t, ten, five, _ = at
                        g, q = 2 * i + (k - 7 - five) // GROUP, ten // GROUP
                        if five == 0:
                            begin(g)
                        if five % 2 == 0:
                            pe.wait_ge(lo_by_pool, 3 * g + five // 2 + 1)
                        else:
                            pe.wait_ge(lo_by_dve, 2 * g + five // 2 + 1)
                        sum_tile(q, q, five)
                    if windows > 1 and (at := group_at(k, i, 11)):
                        g, q = at
                        pe.wait_ge(lo_by_pool, 3 * (g + 1))
                        pe.wait_ge(lo_by_dve, 2 * (g + 1))
                        settle(pe)
                        first = static(g) and g == 0
                        if first:
                            for w in range(2):
                                sums(q, w, w)
                                turn(w)
                        with pe.Fori(1 if first else 0, windows // 2) as w:
                            for v in range(2):
                                sums(q, v, g * windows + 2 * w + v)
                                turn(g * windows + 2 * w + v)
                    if windows == 1 and (at := group_at(k, i, 13)):
                        turn(at[0])

                ticks(pe, tick)

            with pe.If(widest < WIN):
                layer1(1)
            with pe.Else():
                layer1(NWIN)

            def node_tick(k, i):
                if at := node_at(k, i, 0):
                    n, q = at
                    pe.wait_ge(sum_staged, n + 1)
                    if not (static(n) and n < 2):
                        pe.wait_ge(fy_ready, n - 1)
                    for c in range(C):
                        last = pe.transpose(bank[2 + q % 2][0:NODE_TILE, c * P:(c + 1) * P], stage[:, q % 2, c, :],
                                            ident[:, :])
                    last.then_inc(sum_turned, 1)

            node_ticks(pe, node_tick)

        @block.vector
        def _(dve):
            dve.memset(zero[:, :], 0.0).then_inc(consts, 1)
            dve.memset(b2_two[:, :], 0.0).then_inc(consts, 1)
            dve.memset(ones_r[:, :].bitcast(F32), 1.0).then_inc(consts, 1)
            dve.memset(eps[:, :], EPS).then_inc(consts, 1)
            dve.memset(ones_f[:, :], 1.0).then_inc(consts, 1)
            for k in range(2):
                dve.memset(sumT0[:, k, :], 0.0).then_inc(sums_zero, 1)
            dve.wait_ge(edges_in, 48)
            dve.tensor_copy(dst_f[:, :], dst_i[:, :]).then_inc(floats_ready, 1)
            dve.tensor_copy(typ_f[:, :], typ_i[:, :]).then_inc(floats_ready, 1)
            dve.tensor_copy(comp_T[:, :, :], comp_bc[:, :].rearrange("p (r b) -> p b r", r=NR)).then_inc(comp_turned, 1)
            dve.wait_ge(floats_ready, 2)
            by_group = dst_f[:, :].rearrange("p (g j) -> p g j", j=GROUP)
            dve.tensor_reduce(ext[:, 0, 0:G], by_group, AX.X, ALU.min).then_inc(ext_ready, 1)
            dve.tensor_reduce(ext[:, 1, 0:G], by_group, AX.X, ALU.max).then_inc(ext_ready, 1)
            dve.wait_ge(ext_turned, 2)
            dve.tensor_reduce(ext2[0:G, 0:1], bank[0][0:G, 0:P], AX.X, ALU.min).then_inc(ext2_ready, 1)
            dve.tensor_reduce(ext2[0:G, 1:2], bank[1][0:G, 0:P], AX.X, ALU.max).then_inc(ext2_ready, 1)
            dve.wait_ge(ext2_ready, 2)
            dve.tensor_tensor(ext2[0:G, 2:3], ext2[0:G, 1:2], ext2[0:G, 0:1], ALU.subtract).then_inc(span_ready, 1)
            dve.wait_ge(span_ready, 1)
            dve.tensor_copy(ext_wide[0:G, 0, :], ext2[0:G, 0:1].to_broadcast([G, P])).then_inc(wide_ready, 1)
            dve.tensor_copy(ext_wide[0:G, 1, :], ext2[0:G, 2:3].to_broadcast([G, P])).then_inc(wide_ready, 1)
            dve.wait_ge(plan_wide, 2)
            dve.tensor_copy(base_row[0:1, 0:G], bank[2][0:1, 0:G]).then_inc(plan_ready, 1)
            dve.tensor_tensor(dst_rel[:, :].rearrange("p (g j) -> p g j", j=GROUP), by_group,
                              bank[2][:, 0:G].rearrange("p (g o) -> p g o", o=1).to_broadcast([P, G, GROUP]),
                              ALU.subtract).then_inc(rel_ready, 1)
            dve.tensor_reduce(span_f[0:1, 0:1], bank[3][0:1, 0:G], AX.X, ALU.max).then_inc(widest_ready, 1)
            dve.wait_ge(widest_ready, 1)
            dve.tensor_copy(span_i[0:1, 0:1], span_f[0:1, 0:1]).then_inc(plan_ready, 1)
            dve.wait_ge(iota_set, 1)
            dve.tensor_copy(iota[:, :], iota_i[:, :]).then_inc(iota_ready, 1)
            dve.wait_ge(iota_ready, 1)
            dve.wait_ge(rel_ready, 1)
            dve.wait_ge(comp_turned, 1)
            dve.wait_ge(plan_ready, 2)
            widest = dve.value_load(span_i[0:1, 0:1], min_val=0, max_val=N)
            dve.wait_ge(sums_zero, KB)

            def base_of(g):
                at = base_row[0:1, g:g + 1] if static(g) else base_row[0:1, bass.ds(g, 1)]
                return dve.value_load(at, min_val=0, max_val=NPAD - WIN)

            def make_hot(to, g, window, ready):
                shape = [P, GROUP, WIN]
                ends, first = (dst_rel, 0) if window is None else (dst_f, window * WIN)
                return dve.tensor_tensor(
                    to,
                    ends[:, bass.ds(g * GROUP, GROUP)].rearrange("p (j o) -> p j o", o=1).to_broadcast(shape),
                    iota[:, bass.ds(first, WIN)].rearrange("p (o w) -> p o w", o=1).to_broadcast(shape),
                    ALU.is_equal).then_inc(ready, 1)

            def layer0(windows):
                def comp_of_edges(q, g):
                    dve.tensor_tensor(
                        type_hot[:, :, :],
                        typ_f[:, bass.ds(g * GROUP, GROUP)].rearrange("p (j o) -> p j o", o=1).to_broadcast([P, GROUP, NR]),
                        iota[:, 0:NR].rearrange("p (o r) -> p o r", o=1).to_broadcast([P, GROUP, NR]),
                        ALU.is_equal).then_inc(type_hot_ready, 1)
                    dve.wait_ge(type_hot_ready, g + 1)
                    shape = [P, GROUP, NB, NR]
                    dve.tensor_tensor(
                        comp_prod[:, :, :, :],
                        type_hot[:, :, :].rearrange("p j (o r) -> p j o r", o=1).to_broadcast(shape),
                        comp_T[:, :, :].rearrange("p (o b) r -> p o b r", o=1).to_broadcast(shape),
                        ALU.mult).then_inc(comp_prod_ready, 1)
                    dve.wait_ge(comp_prod_ready, g + 1)
                    dve.tensor_reduce(comp_e[:, q, :, :], comp_prod[:, :, :, :], AX.X, ALU.add).then_inc(comp_e_ready, 1)
                    dve.wait_ge(comp_e_ready, g + 1)

                def weigh(q, slot, g, s, window, first):
                    make_hot(hot[:, slot, :, :], g, window, hot0_ready)
                    dve.wait_ge(hot0_ready, s + 1)
                    if not first:
                        dve.wait_ge(sum0_ready, s - 1)
                    shape = [P, GROUP, NB, WIN]
                    dve.tensor_tensor(
                        whot[:, slot, :, :, :],
                        hot[:, slot, :, :].rearrange("p j (o w) -> p j o w", o=1).to_broadcast(shape),
                        comp_e[:, q, :, :].rearrange("p j (b o) -> p j b o", o=1).to_broadcast(shape),
                        ALU.mult).then_inc(whot_ready, 1)

                def add(slot, s, base):
                    dve.wait_ge(sum0_ready, s + 1)
                    if not (static(s) and s == 0):
                        dve.wait_ge(sum0_added, s)
                    to = sumT0[:, :, bass.ds(base, WIN)]
                    dve.tensor_tensor(to, to, bank[6 + slot][:, 0:KB * WIN].rearrange("p (k w) -> p k w", k=KB),
                                      ALU.add).then_inc(sum0_added, 1)

                def release_rows():
                    dve.sem_inc(x_used, 1)

                if windows == 1:
                    def group(q, g, i):
                        comp_of_edges(q % 2, g)
                        weigh(q % 2, q % 2, g, g, None, static(g) and g < 2)
                        if not (static(g) and g == 0):
                            add(1 - q % 2, g - 1, base_of(g - 1))
                            release_rows()

                    rounds(dve, RING0, group)
                    add((G - 1) % 2, G - 1, base_of(G - 1))
                    release_rows()
                else:
                    def group(q, g, i):
                        comp_of_edges(q % 2, g)
                        settle(dve)
                        first = static(g) and g == 0
                        if first:
                            for w in range(2):
                                weigh(0, w, g, w, w, True)
                                add(w, w, w * WIN)
                        with dve.Fori(1 if first else 0, windows // 2) as w:
                            for v in range(2):
                                s = g * windows + 2 * w + v
                                weigh(q % 2, v, g, s, 2 * w + v, False)
                                add(v, s, (2 * w + v) * WIN)
                        release_rows()

                    rounds(dve, RING0, group)
                dve.wait_ge(sum0_added, G * windows)
                dve.sem_inc(layer0_summed, 1)

            with dve.If(widest < WIN):
                layer0(1)
            with dve.Else():
                layer0(NWIN)

            dve.wait_ge(weights_in, 16 * 16)
            dve.wait_ge(b2_in, 16)
            dve.wait_ge(sums_zero, KB + C)
            dve.tensor_copy(we_hi[:, :], we[:, :]).then_inc(w_hi, 1)
            dve.tensor_copy(w2_hi[:, :, :], w2[:, :, :]).then_inc(w_hi, 1)
            dve.tensor_copy(b2_r[:, :], b2_two[:, :]).then_inc(w_hi, 1)
            dve.wait_ge(w_hi, 3)
            dve.tensor_tensor(we_lo[:, :], we[:, :], we_hi[:, :].bitcast(F32), ALU.subtract).then_inc(split_w, 2)
            dve.tensor_tensor(w2_lo[:, :, :], w2[:, :, :], w2_hi[:, :, :].bitcast(F32), ALU.subtract).then_inc(split_w, 2)
            dve.tensor_tensor(b2_r[32:33, :], b2_two[32:33, :], b2_r[32:33, :].bitcast(F32),
                              ALU.subtract).then_inc(split_w, 2)

            T = NODE_TILE

            def mixed_rows(q, n):
                dve.wait_ge(mixed, n + 1)
                own_root = (root[0:T, n, :] if static(n) else
                            root[0:T, bass.ds(n, 1), :].rearrange("p o n -> p (o n)"))
                dve.tensor_tensor(y[0:T, q, :], bank[q][0:T, 0:D], own_root, ALU.add).then_inc(y_ready, 1)
                dve.wait_ge(y_ready, n + 1)
                dve.bn_stats(stats[0:T, q, :], y[0:T, q, :]).then_inc(stats_ready, 1)
                dve.wait_ge(stats_ready, n + 1)
                settle(dve)
                dve.bn_aggr(mv[0:T, q, :], stats[0:T, q, :]).then_inc(var_ready, 1)

            def node_tile(q, n, i):
                if not (static(n) and n < 2):
                    dve.wait_ge(x1_out[q], 16 * i)
                    dve.wait_ge(x1_turned, n - 1)
                dve.wait_ge(std_ready, n + 1)
                dve.reciprocal(rstd[0:T, q, :], std[0:T, q, :]).then_inc(rstd_ready, 1)
                dve.wait_ge(rstd_ready, n + 1)
                dve.tensor_scalar(x1_s[0:T, q, :], y[0:T, q, :], mv[0:T, q, 0:1], rstd[0:T, q, 0:1], ALU.subtract,
                                  ALU.mult).then_inc(x1_ready, 1)
                if not (static(n) and n >= NT - 1):
                    mixed_rows(1 - q, n + 1)
                dve.wait_ge(table_mm, n + 1)
                if not (static(n) and n < 2):
                    dve.wait_ge(table_out[q], 16 * i)
                dve.tensor_tensor(table_s[0:T, q, :], bank[4 + q][0:T, :], bx_bc[0:T, :], ALU.add).then_inc(table_ready, 1)

            dve.wait_ge(root_kept, NT)
            mixed_rows(0, 0)
            node_pairs(dve, node_tile)

            def split_lo(g, q, half):
                dve.wait_ge(edge_hi, g + 1)
                at = slice(half * GE // 2, (half + 1) * GE // 2)
                dve.tensor_tensor(edge_r[DE:P, q, at], edge_f[DE:P, q, at], edge_r[DE:P, q, at].bitcast(F32),
                                  ALU.subtract).then_inc(edge_split, 1)

            def layer1(windows):
                split_lo(0, 0, 0)
                split_lo(0, 0, 1)

                def hot1(slot, g, s, window, first):
                    if not first:
                        dve.wait_ge(sum1_ready, s - 1)
                    make_hot(hot_r[:, slot, :, :], g, window, hot1_ready)

                def add(s, base):
                    dve.wait_ge(sum1_turned, s + 1)
                    if not (static(s) and s == 0):
                        dve.wait_ge(sum1_added, s)
                    to = sumT1[:, :, bass.ds(base, WIN)]
                    dve.tensor_tensor(to, to, bank[7][:, 0:C * WIN].rearrange("p (c w) -> p c w", c=C),
                                      ALU.add).then_inc(sum1_added, 1)

                def tick(k, i):
                    for half, ahead in ((0, 4), (1, 2)):
                        if at := group_at(k, i, -ahead):
                            split_lo(*at, half)
                    if at := tile_at(k, i, 0):
                        t, ten, _, two = at
                        dve.wait_ge(row_in[ten], 16 * (i + 1))
                        dve.wait_ge(z_ready, t + 1)
                        dve.tensor_tensor(rows[:, ten, :], bank[two][:, :], rows[:, ten, :], ALU.add).then_inc(pre_ready, 1)
                    added = group_at(k, i, 15) if windows == 1 else None
                    if added:
                        base = base_of(added[0])
                    if at := tile_at(k, i, 2):
                        t, _, five, two = at
                        dve.wait_ge(hi_ready, t + 1)
                        dve.scalar_tensor_tensor(out=h_lo[:, five, :], in0=bank[2 + two][:, 0:D], scalar=0.0,
                                                 in1=h_hi[:, five, :].bitcast(F32), op0=ALU.max,
                                                 op1=ALU.subtract).then_inc(lo_ready, 1)
                    if at := tile_at(k, i, 4):
                        t, ten, five, two = at
                        if not (static(t) and t < GROUP):
                            g = 2 * i + (k - 4 - five) // GROUP
                            if five % 2 == 0:
                                dve.wait_ge(lo_by_pool, 3 * (g - 1) + five // 2 + 1)
                            else:
                                dve.wait_ge(lo_by_dve, 2 * (g - 1) + five // 2 + 1)
                        dve.wait_ge(gate_ready, t + 1)
                        dve.wait_ge(core_ready, t + 1)
                        dve.tensor_tensor(msg[:, five, :], rows[:, ten, D:2 * D], bank[4 + two][:, 0:D],
                                          ALU.mult).then_inc(msg_ready, 1)
                    at = tile_at(k, i, 6)
                    if at and at[2] % 2 == 1:
                        t, ten, five, _ = at
                        dve.wait_ge(msg_hi_ready, t + 1)
                        dve.tensor_tensor(msg_lo[:, ten, :], msg[:, five, :], msg_hi[:, ten, :].bitcast(F32),
                                          ALU.subtract).then_inc(lo_by_dve, 1)
                    if windows == 1:
                        if at := group_at(k, i, 5):
                            g, q = at
                            hot1(q, g, g, None, static(g) and g < 2)
                        if added:
                            add(added[0], base)
                    elif at := group_at(k, i, 11):
                        g, q = at
                        settle(dve)
                        first = static(g) and g == 0
                        if first:
                            for w in range(2):
                                hot1(w, g, w, w, True)
                                add(w, w * WIN)
                        with dve.Fori(1 if first else 0, windows // 2) as w:
                            for v in range(2):
                                s = g * windows + 2 * w + v
                                hot1(v, g, s, 2 * w + v, False)
                                add(s, (2 * w + v) * WIN)

                ticks(dve, tick)
                dve.wait_ge(sum1_added, G * windows)
                dve.sem_inc(layer1_summed, 1)

            with dve.If(widest < WIN):
                layer1(1)
            with dve.Else():
                layer1(NWIN)

            def variance(h, n, q, of):
                dve.bn_stats(f_stats[0:T, h, q, :], of).then_inc(fstats_ready[h], 1)
                dve.wait_ge(fstats_ready[h], n + 1)
                settle(dve)
                dve.bn_aggr(f_mv[0:T, h, q, :], f_stats[0:T, h, q, :]).then_inc(fvar_ready[h], 1)

            def scale_and_shift(h, n, q):
                dve.wait_ge(fstd_ready[h], n + 1)
                dve.reciprocal(f_rstd[0:T, h, q:q + 1], f_std[0:T, h, q:q + 1]).then_inc(frstd_ready[h], 1)
                dve.wait_ge(frstd_ready[h], n + 1)
                dve.scalar_tensor_tensor(out=f_shift[0:T, h, q:q + 1], in0=f_mv[0:T, h, q, 0:1], scalar=-1.0,
                                         in1=f_rstd[0:T, h, q:q + 1], op0=ALU.mult,
                                         op1=ALU.mult).then_inc(fshift_ready[h], 1)

            def node_tick(k, i):
                if at := node_at(k, i, 1):
                    scale_and_shift(0, *at)
                if at := node_at(k, i, 3):
                    scale_and_shift(1, *at)
                if at := node_at(k, i, 0):
                    n, q = at
                    dve.wait_ge(sum_turned, n + 1)
                    dve.wait_ge(x1_in[q], 16 * (i + 1))
                    dve.tensor_tensor(f_y[0:T, q, :], bank[2 + q % 2][0:T, 0:D], f_x[0:T, q, :],
                                      ALU.add).then_inc(fy_ready, 1)
                    dve.wait_ge(fy_ready, n + 1)
                    variance(0, n, q, f_y[0:T, q, :])
                if at := node_at(k, i, 2):
                    n, q = at
                    dve.wait_ge(fnorm_ready[0], n + 1)
                    dve.tensor_tensor(f_z[0:T, q, :], f_w[0:T, q, :], gamma_bc[0:T, :], ALU.mult).then_inc(fz_ready, 1)
                    dve.wait_ge(fz_ready, n + 1)
                    dve.wait_ge(fxb_ready, n + 1)
                    if not (static(n) and n < RING_F):
                        dve.wait_ge(fnorm_ready[1], n - (RING_F - 1))
                    dve.tensor_tensor(f_r[0:T, q, :], f_z[0:T, q, :], f_xb[0:T, q, :], ALU.add).then_inc(fr_ready, 1)
                    dve.wait_ge(fr_ready, n + 1)
                    variance(1, n, q, f_r[0:T, q, :])

            node_ticks(dve, node_tick)


def kernel(x, src, dst, edge_attr_64, edge_type_8, L0_gnn_basis, L0_gnn_comp, L0_gnn_loop_weight,
           L0_gnn_bias_param, L1_gnn_W1, L1_gnn_b1, L1_gnn_W2, L1_gnn_b2, L1_gnn_Wg, L1_gnn_bg,
           L1_gnn_gamma, L1_gnn_beta):
    import numpy as np
    import concourse.bacc as bacc
    from concourse.bass_utils import run_bass_kernel_spmd

    x = np.asarray(x)
    N, D = x.shape
    E = np.asarray(src).shape[0]
    tiles = E // P

    def laid(a):
        return np.ascontiguousarray(np.asarray(a))

    arrays = {
        "x": laid(x),
        "xT": laid(x.T.reshape(D // P, P, N).transpose(1, 0, 2)),
        "src": laid(np.asarray(src).reshape(tiles // GROUP, GROUP, P).transpose(0, 2, 1)),
        "dst": laid(np.asarray(dst).reshape(tiles, P).T),
        "etype": laid(np.asarray(edge_type_8).reshape(tiles, P).T),
        "edge_T": laid(np.asarray(edge_attr_64).T),
        "basis": laid(L0_gnn_basis), "comp": laid(L0_gnn_comp), "loop_w": laid(L0_gnn_loop_weight),
        "bias0": laid(L0_gnn_bias_param), "W1": laid(L1_gnn_W1), "b1": laid(L1_gnn_b1), "W2": laid(L1_gnn_W2),
        "b2": laid(L1_gnn_b2), "Wg": laid(L1_gnn_Wg), "bg": laid(L1_gnn_bg), "gamma": laid(L1_gnn_gamma),
        "beta": laid(L1_gnn_beta),
    }
    nc = bacc.Bacc("TRN2", target_bir_lowering=False, num_devices=1)
    args = {name: nc.dram_tensor(f"in_{name}", a.shape, mybir.dt.from_np(a.dtype), kind="ExternalInput").ap()
            for name, a in arrays.items()}
    out = nc.dram_tensor("out_rows", [N, D], F32, kind="ExternalOutput").ap()
    build(nc, **args, out=out)
    r = run_bass_kernel_spmd(nc, [{f"in_{name}": a for name, a in arrays.items()}], core_ids=[0])
    return r.results[0]["out_rows"]
```

```python
from contextlib import ExitStack

import concourse.bass as bass
from concourse import mybir

F32 = mybir.dt.float32
F32R = mybir.dt.float32r
I32 = mybir.dt.int32
ALU = mybir.AluOpType
ACT = mybir.ActivationFunctionType
AX = mybir.AxisListType

P = 128
GROUP = 5
RING0 = 5
PERIOD = 25
NODES_PER = 4
DRAIN0 = 12
BATCH = 4
WIN = 32
NODE_TILE = 125
EPS = 1e-5


def build(nc, x, xT, src, dst, etype, edge_T, basis, comp, loop_w, bias0,
          W1, b1, W2, b2, Wg, bg, gamma, beta, out):
    N, D = x.shape
    G = src.shape[0]
    TILES = G * GROUP
    DE = edge_T.shape[0]
    NB, NR = basis.shape[0], comp.shape[0]
    C = D // P
    NT = N // NODE_TILE
    PAIRS = G // 2
    NWIN = 2 * -(-N // (2 * WIN))
    NPAD = NWIN * WIN
    KB = C * NB
    BATCHES = NT // BATCH
    assert G % 2 == 1 and NT * NODE_TILE == N and NT % BATCH == 0 and 2 * DE == P and KB == 8
    assert G == NT // NODES_PER * PERIOD and BATCH == NODES_PER and PERIOD == RING0 * (NODES_PER + 1)
    GE = GROUP * P

    h_table = nc.dram_tensor("node_table", [N, 2 * D], F32, kind="Internal").ap()
    x1_dram = nc.dram_tensor("x1_rows", [N, D], F32, kind="Internal").ap()
    xb_dram = nc.dram_tensor("x1_beta_rows", [N, D], F32, kind="Internal").ap()

    ctx = ExitStack()
    with ctx:
        def sb(name, shape, dt=F32):
            return ctx.enter_context(nc.sbuf_tensor(name, shape, dt))

        def sem(name):
            return ctx.enter_context(nc.semaphore(name))

        bank = [ctx.enter_context(nc.psum_tensor(f"bank{i}", [P, 512], F32)) for i in range(8)]

        ident = sb("ident", [P, P])
        iota = sb("iota", [P, NPAD])
        ones_r = sb("ones_r", [64, P], F32R)
        zero = sb("zero", [P, 1])
        dst_f = sb("dst_f", [P, TILES])
        typ_f = sb("typ_f", [P, TILES])
        dst_rel = sb("dst_rel", [P, TILES])
        src_slot = sb("src_slot", [P, RING0, GROUP], I32)
        ext = sb("ext", [P, 2, P])
        ext2 = sb("ext2", [P, 4])
        ext_wide = sb("ext_wide", [P, 2, P])
        base_row = sb("base_row", [1, P], I32)
        span_f = sb("span_f", [1, 2])
        span_i = sb("span_i", [1, 2], I32)
        basis_sb = sb("basis_sb", [P, KB, D])
        loop_sb = sb("loop_sb", [P, C, D])
        comp_bc = sb("comp_bc", [P, NR * NB])
        comp_T = sb("comp_T", [P, NB, NR])
        bias0_row = sb("bias0_row", [1, D])
        ones_f = sb("ones_f", [1, P])
        wx = sb("wx", [P, C, 2 * D])
        bx_bc = sb("bx_bc", [P, 2 * D])
        we = sb("we", [P, 2 * D])
        we_hi = sb("we_hi", [P, 2 * D], F32R)
        we_lo = sb("we_lo", [P, 2 * D], F32R)
        w2 = sb("w2", [P, C, D])
        w2_hi = sb("w2_hi", [P, C, D], F32R)
        w2_lo = sb("w2_lo", [P, C, D], F32R)
        b2_two = sb("b2_two", [64, D])
        b2_r = sb("b2_r", [64, D], F32R)
        gamma_bc = sb("gamma_bc", [P, D])
        beta_bc = sb("beta_bc", [P, D])
        sumT1 = sb("sumT1", [P, C, NPAD])
        hot_r = sb("hot_r", [P, 2, GROUP, WIN], F32R)

        xT_s = sb("xT_s", [P, C, NODE_TILE])
        stats = sb("stats", [P, 6])
        mv = sb("mv", [P, 2])
        std = sb("std", [P, 1])
        rstd = sb("rstd", [P, 1])
        late = sb("late", [1, G])
        late_f = sb("late_f", [1, 2])
        eps = sb("eps", [P, 1])

        ctx0 = ExitStack()
        with ctx0:
            def sb0(name, shape, dt=F32):
                return ctx0.enter_context(nc.sbuf_tensor(name, shape, dt))

            sumT0 = sb0("sumT0", [P, KB, NPAD])
            x_rows = sb0("x_rows", [P, RING0 * GROUP, D])
            hot = sb0("hot", [P, GROUP, WIN])
            type_hot = sb0("type_hot", [P, GROUP, NR])
            comp_prod = sb0("comp_prod", [P, GROUP, NB, NR])
            comp_e = sb0("comp_e", [P, GROUP, NB])
            x1_s = sb0("x1_s", [P, D])
            xb_s = sb0("xb_s", [P, D])
            with ExitStack() as ctx_i:
                iota_i = ctx_i.enter_context(nc.sbuf_tensor("iota_i", [P, NPAD], I32))
                dst_i = ctx_i.enter_context(nc.sbuf_tensor("dst_i", [P, TILES], I32))
                typ_i = ctx_i.enter_context(nc.sbuf_tensor("typ_i", [P, TILES], I32))
            whot = sb0("whot", [P, 3, GROUP, NB, WIN])
            stage = sb0("stage", [P, KB, NODE_TILE])
            table_s = sb0("table_s", [P, 2 * D])
            x1T = sb0("x1T", [P, C, NODE_TILE])
        edge_f = sb("edge_f", [P, 2, GE])
        edge_r = sb("edge_r", [P, 2, GE], F32R)
        h_hi = sb("h_hi", [P, GROUP, D], F32R)
        h_lo = sb("h_lo", [P, GROUP, D], F32R)
        msg = sb("msg", [P, GROUP, D])
        msg_hi = sb("msg_hi", [P, 2 * GROUP, D], F32R)
        msg_lo = sb("msg_lo", [P, 2 * GROUP, D], F32R)
        sum_rows = sb("sum_rows", [WIN, D])
        f_x = sb("f_x", [P, NT, D])
        f_xb = sb("f_xb", [P, NT, D])
        f_sum = sb("f_sum", [P, 2, C, BATCH * NODE_TILE])
        rows = sb("rows", [P, 2 * GROUP, 2 * D])
        f_stats = sb("f_stats", [P, BATCH, 6])
        f_mv = sb("f_mv", [P, 2, NT, 2])
        f_std = sb("f_std", [P, 2, NT, 1])
        f_rstd = sb("f_rstd", [P, 2, NT, 1])
        f_shift = sb("f_shift", [P, 2, NT, 1])

        ident_set, iota_set, consts = sem("ident_set"), sem("iota_set"), sem("consts")
        edges_in, weights_in, b2_in = sem("edges_in"), sem("weights_in"), sem("b2_in")
        pool_zeroed, floats_ready, iota_ready, rel_ready = (
            sem("pool_zeroed"), sem("floats_ready"), sem("iota_ready"), sem("rel_ready"))
        ext_ready, ext_turned, ext2_ready, span_ready, wide_ready, plan_wide, widest_ready, plan_ready = (
            sem("ext_ready"), sem("ext_turned"), sem("ext2_ready"), sem("span_ready"), sem("wide_ready"),
            sem("plan_wide"), sem("widest_ready"), sem("plan_ready"))
        sums_zero, comp_turned, split_w, w_hi = sem("sums_zero"), sem("comp_turned"), sem("split_w"), sem("w_hi")
        src0_in = [sem(f"src0_in{q}") for q in range(RING0)]
        x_in = [sem(f"x_in{q}") for q in range(RING0)]
        x_used = sem("x_used")
        type_hot_ready, comp_prod_ready, comp_e_ready = (
            sem("type_hot_ready"), sem("comp_prod_ready"), sem("comp_e_ready"))
        hot0_ready, whot_ready, sum0_ready, sum0_added, layer0_summed = (
            sem("hot0_ready"), sem("whot_ready"), sem("sum0_ready"), sem("sum0_added"), sem("layer0_summed"))
        late_ready, late_max_ready, late_flag_ready = sem("late_ready"), sem("late_max_ready"), sem("late_flag_ready")
        xT_in = sem("xT_in")
        staged, mixed, stats_ready, var_ready, std_ready, rstd_ready = (
            sem("staged"), sem("mixed"), sem("stats_ready"), sem("var_ready"), sem("std_ready"), sem("rstd_ready"))
        x1_ready, x1_turned, x1T_ready = sem("x1_ready"), sem("x1_turned"), sem("x1T_ready")
        table_mm, table_ready = sem("table_mm"), sem("table_ready")
        x1_out, table_out, xb_ready, xb_out = sem("x1_out"), sem("table_out"), sem("xb_ready"), sem("xb_out")
        src1_in = [sem(f"src1_in{q}") for q in range(2)]
        edge_in = [sem(f"edge_in{q}") for q in range(2)]
        edge_hi, edge_split = sem("edge_hi"), sem("edge_split")
        row_in = [sem(f"row_in{q}") for q in range(2 * GROUP)]
        z_ready, pre_ready, gate_ready, turned = (
            sem("z_ready"), sem("pre_ready"), sem("gate_ready"), sem("turned"))
        hi_ready, lo_ready, core_ready, msg_ready = (
            sem("hi_ready"), sem("lo_ready"), sem("core_ready"), sem("msg_ready"))
        msg_hi_ready, lo_by_pool, lo_by_dve = sem("msg_hi_ready"), sem("lo_by_pool"), sem("lo_by_dve")
        hot1_ready, sum1_ready, sum1_kept, sum1_turned, sum1_added, layer1_summed = (
            sem("hot1_ready"), sem("sum1_ready"), sem("sum1_kept"), sem("sum1_turned"), sem("sum1_added"),
            sem("layer1_summed"))
        x1_in, xb_in = sem("x1_in"), sem("xb_in")
        sum_staged, sum_turned, y_ready, fz_ready, fr_ready = (
            sem(s) for s in ("sum_staged", "sum_turned", "y_ready", "fz_ready", "fr_ready"))
        fstats_ready, fvar_ready, fstd_ready, frstd_ready, fshift_ready = (
            [sem(f"{s}{h}") for h in range(2)]
            for s in ("fstats_ready", "fvar_ready", "fstd_ready", "frstd_ready", "fshift_ready"))
        normed, out_by_act, out_by_pool = sem("normed"), sem("out_by_act"), sem("out_by_pool")
        passed = sem("passed")
        out_done = sem("out_done")

        def static(v):
            return isinstance(v, int)

        def rounds(eng, ring, step):
            for q in range(ring):
                step(q, q, 0)
            with eng.Fori(1, G // ring) as i:
                for q in range(ring):
                    step(q, ring * i + q, i)
            for q in range(G % ring):
                step(q, G - G % ring + q, G // ring)

        def slot0(q):
            return (0, 1, 0, 1, 2)[q % RING0]

        def periods(eng, step):
            for u in range(PERIOD):
                step(u, 0)
            with eng.Fori(1, G // PERIOD) as i:
                for u in range(PERIOD):
                    step(u, i)
            for u in range(DRAIN0):
                step(u, G // PERIOD)

        def group0_at(u, i):
            if static(i) and i >= G // PERIOD:
                return None
            return PERIOD * i + u, u % RING0

        def node0_at(u, i, lag):
            v = u - lag
            if v < 0:
                v, i = v + PERIOD, i - 1
            if v % RING0 or v == 0:
                return None
            n = NODES_PER * i + v // RING0 - 2
            return None if static(n) and not 0 <= n < NT else n

        def groups_before(i, m):
            return PERIOD * i + RING0 * (m + 2 + (m == NODES_PER - 1))

        def batch_times(lag):
            return range(BATCHES + lag)

        def batch_at(time, lag):
            return time - lag if 0 <= time - lag < BATCHES else None

        def in_batch(b):
            return slice(BATCH * b, BATCH * (b + 1))

        def pair_bank(pair):
            return bank[pair % 6][0:NODE_TILE, 0:2 * D]

        def ticks(eng, tick):
            for i in range(2):
                for k in range(2 * GROUP):
                    tick(k, i)
            with eng.Fori(2, PAIRS) as i:
                for k in range(2 * GROUP):
                    tick(k, i)
            for k in range(3 * GROUP + 1):
                tick(k, PAIRS)

        def tile_at(k, i, lag):
            if static(i) and not 0 <= 2 * GROUP * i + k - lag < TILES:
                return None
            return 2 * GROUP * i + (k - lag), (k - lag) % (2 * GROUP), (k - lag) % GROUP, (k - lag) % 2

        def group_at(k, i, lag):
            at = tile_at(k, i, lag)
            if at is None or (k - lag) % GROUP:
                return None
            return 2 * i + (k - lag) // GROUP, ((k - lag) // GROUP) % 2

        def settle(eng):
            eng.sem_inc(passed, 1)

        def nodes(n):
            return bass.ds(n * NODE_TILE, NODE_TILE)

        block = ctx.enter_context(nc.Block())

        @block.sync
        def _(sp):
            sp.dma_start(dst_i[:, :], dst).then_inc(edges_in, 16)
            sp.dma_start(typ_i[:, :], etype).then_inc(edges_in, 16)
            sp.dma_start(comp_bc[:, :],
                         comp.rearrange("(o r) b -> o (r b)", o=1).to_broadcast([P, NR * NB])).then_inc(edges_in, 16)

            def load_src0(q, g, i):
                if not (static(g) and g < RING0):
                    sp.wait_ge(x_in[q], 16 * GROUP * i)
                sp.dma_start(src_slot[:, q, :], src[g, :, :]).then_inc(src0_in[q], 16)

            rounds(sp, RING0, load_src0)

            sp.wait_ge(layer0_summed, 1)
            sp.wait_ge(staged, NT)

            def load_edges(q, g, i):
                if not (static(g) and g < 2):
                    for j in range(GROUP):
                        sp.wait_ge(row_in[q * GROUP + j], 16 * i)
                sp.dma_start(src_slot[:, q, :], src[g, :, :]).then_inc(src1_in[q], 16)
                if not (static(g) and g < 2):
                    sp.wait_ge(edge_split, 2 * (g - 1))
                for half in range(2):
                    sp.dma_start(edge_f[half * DE:(half + 1) * DE, q, :],
                                 edge_T[:, bass.ds(g * GE, GE)]).then_inc(edge_in[q], 16)

            def by_tile(rows_dram):
                return rows_dram.rearrange("(n p) d -> p n d", p=NODE_TILE)

            third = PAIRS // 3
            for q in range(2):
                load_edges(q, q, 0)
            for at in range(3):
                with sp.Fori(max(1, at * third), PAIRS if at == 2 else (at + 1) * third) as i:
                    for q in range(2):
                        load_edges(q, 2 * i + q, i)
                if at == 0:
                    sp.wait_ge(x1_out, 16 * NT)
                    sp.dma_start(f_x[0:NODE_TILE, :, :], by_tile(x1_dram)).then_inc(x1_in, 16)
                if at == 1:
                    sp.wait_ge(xb_out, 16 * NT)
                    sp.dma_start(f_xb[0:NODE_TILE, :, :], by_tile(xb_dram)).then_inc(xb_in, 16)
            load_edges(0, G - 1, PAIRS)

            for b in range(BATCHES):
                sp.wait_ge(out_by_act, BATCH // 2 * (b + 1))
                sp.wait_ge(out_by_pool, BATCH // 2 * (b + 1))
                sp.dma_start(by_tile(out)[:, in_batch(b), :], f_x[0:NODE_TILE, in_batch(b), :]).then_inc(out_done, 16)
            sp.wait_ge(out_done, 16 * BATCHES)

        @block.gpsimd
        def _(pool):
            pool.memset(ident[:, :], 0.0).then_inc(pool_zeroed, 1)
            pool.iota(iota_i[:, :], [[1, NPAD]], base=0, channel_multiplier=0).then_inc(iota_set, 1)
            pool.wait_ge(pool_zeroed, 1)
            pool.affine_select(out=ident[:, :], in_=ident[:, :], compare_op=ALU.not_equal, fill=1.0,
                               base=0, pattern=[[-1, P]], channel_multiplier=1).then_inc(ident_set, 1)

            def gather_x(q, g, i):
                pool.wait_ge(src0_in[q], 16 * (i + 1))
                if not (static(g) and g < RING0):
                    pool.wait_ge(x_used, g - (RING0 - 1))
                    settle(pool)
                for j in range(GROUP):
                    pool.indirect_dma_start(
                        out=x_rows[:, q * GROUP + j, :], out_offset=None, in_=x,
                        in_offset=bass.IndirectOffsetOnAxis(ap=src_slot[:, q, j:j + 1], axis=0)).then_inc(x_in[q], 16)

            rounds(pool, RING0, gather_x)

            pool.wait_ge(table_out, 16 * NT)
            pool.wait_ge(x1_out, 16 * NT)
            pool.wait_ge(xb_out, 16 * NT)

            def gather_row(k, i, lag):
                t, ten, five, _ = tile_at(k, i, lag)
                if at := group_at(k, i, lag):
                    pool.wait_ge(src1_in[at[1]], 16 * (i + (k - lag) // (2 * GROUP) + 1))
                    settle(pool)
                if not (static(t) and t < 2 * GROUP):
                    pool.wait_ge(msg_ready, t - (2 * GROUP - 1))
                    settle(pool)
                pool.indirect_dma_start(
                    out=rows[:, ten, :], out_offset=None, in_=h_table,
                    in_offset=bass.IndirectOffsetOnAxis(ap=src_slot[:, ten // GROUP, five:five + 1], axis=0)
                ).then_inc(row_in[ten], 16)

            def tick(k, i):
                if tile_at(k, i, -GROUP):
                    gather_row(k, i, -GROUP)
                at = tile_at(k, i, 6)
                if at and at[2] % 2 == 0:
                    t, ten, five, _ = at
                    pool.wait_ge(msg_hi_ready, t + 1)
                    pool.tensor_tensor(msg_lo[:, ten, :], msg[:, five, :], msg_hi[:, ten, :].bitcast(F32),
                                       ALU.subtract).then_inc(lo_by_pool, 1)

            for t in range(GROUP):
                gather_row(t, 0, 0)
            ticks(pool, tick)

            pool.wait_ge(weights_in, 16 * 16)
            T = NODE_TILE
            for time in batch_times(3):
                if (b := batch_at(time, 3)) is not None:
                    pool.wait_ge(fshift_ready[1], b + 1)
                    for n in range(BATCH * b + BATCH // 2, BATCH * (b + 1)):
                        pool.tensor_scalar(f_x[0:T, n, :], f_x[0:T, n, :], f_rstd[0:T, 1, n, :], f_shift[0:T, 1, n, :],
                                           ALU.mult, ALU.add).then_inc(out_by_pool, 1)
                if (b := batch_at(time, 0)) is not None:
                    pool.wait_ge(normed, BATCH * (b + 1))
                    pool.tensor_tensor(
                        f_x[0:T, in_batch(b), :], f_x[0:T, in_batch(b), :],
                        gamma_bc[0:T, :].rearrange("p (o d) -> p o d", o=1).to_broadcast([T, BATCH, D]),
                        ALU.mult).then_inc(fz_ready, 1)

        @block.scalar
        def _(act):
            def row(v, n):
                return v.rearrange("(o n) -> o n", o=1).to_broadcast([P, n])

            act.wait_ge(consts, 5)
            for k in range(2, KB):
                act.activation(sumT0[:, k, :], zero[:, 0:1].to_broadcast([P, NPAD]), ACT.Copy).then_inc(sums_zero, 1)
            b2_row = b2.rearrange("(o n) -> o n", o=1)
            for to, at in [
                (loop_sb[:, :, :], loop_w.rearrange("(c p) n -> p c n", p=P)),
                (bias0_row[:, :], bias0.rearrange("(o n) -> o n", o=1)),
                (basis_sb[:, 0:NB, :], basis[:, 0:P, :].rearrange("b p n -> p b n")),
                (basis_sb[:, NB:KB, :], basis[:, P:D, :].rearrange("b p n -> p b n")),
                (wx[:, :, 0:D], W1[0:D, :].rearrange("(c p) n -> p c n", p=P)),
                (wx[:, :, D:2 * D], Wg[0:D, :].rearrange("(c p) n -> p c n", p=P)),
                (bx_bc[:, 0:D], row(b1, D)),
                (bx_bc[:, D:2 * D], row(bg, D)),
                (we[0:DE, 0:D], W1[D:D + DE, :]),
                (we[DE:P, 0:D], W1[D:D + DE, :]),
                (we[0:DE, D:2 * D], Wg[D:D + DE, :]),
                (we[DE:P, D:2 * D], Wg[D:D + DE, :]),
                (w2[:, :, :], W2.rearrange("(c p) n -> p c n", p=P)),
                (gamma_bc[:, :], row(gamma, D)),
                (beta_bc[:, :], row(beta, D)),
                (b2_two[0:1, :], b2_row),
            ]:
                act.dma_start(to, at).then_inc(weights_in, 16)
            act.dma_start(b2_two[32:33, :], b2_row).then_inc(b2_in, 16)
            for c in range(C):
                act.activation(sumT1[:, c, :], zero[:, 0:1].to_broadcast([P, NPAD]), ACT.Copy).then_inc(sums_zero, 1)

            act.wait_ge(plan_ready, 2)
            widest = act.value_load(span_i[0:1, 0:1], min_val=0, max_val=N)
            T = NODE_TILE

            def begin(n):
                if not (static(n) and n == 0):
                    act.wait_ge(mixed, n)
                act.activation(stage[:, :, :], sumT0[:, :, nodes(n)], ACT.Copy).then_inc(staged, 1)

            def load_xT(n):
                act.dma_start(xT_s[:, :, :], xT[:, :, nodes(n)]).then_inc(xT_in, 16)

            def dense(n):
                act.wait_ge(mixed, n + 1)
                if not (static(n) and n == NT - 1):
                    load_xT(n + 1)
                act.wait_ge(var_ready, n + 1)
                act.activation(std[0:T, :], mv[0:T, 1:2], ACT.Sqrt, bias=eps[0:T, 0:1]).then_inc(std_ready, 1)
                act.wait_ge(x1_ready, n + 1)
                act.dma_start(x1_dram[nodes(n), :], x1_s[0:T, :]).then_inc(x1_out, 16)
                act.wait_ge(x1_turned, n + 1)
                if not (static(n) and n == 0):
                    act.wait_ge(table_mm, n)
                act.activation(x1T[:, :, :].rearrange("p c n -> p (c n)"), bank[1][:, 0:C * T],
                               ACT.Copy).then_inc(x1T_ready, 1)

            def store_table(n):
                act.wait_ge(xb_ready, n + 1)
                act.dma_start(xb_dram[nodes(n), :], xb_s[0:T, :]).then_inc(xb_out, 16)
                act.wait_ge(table_ready, n + 1)
                act.dma_start(h_table[nodes(n), :], table_s[0:T, :]).then_inc(table_out, 16)

            load_xT(0)
            with act.If(widest < WIN):
                def tile(n, i, m):
                    dense(n)
                    if not (static(n) and n == NT - 1):
                        i, m = (i, m + 1) if m < NODES_PER - 1 else (i + 1, 0)
                        before = groups_before(i, m)
                        act.wait_ge(sum0_added, min(before, G) if static(before) else before)
                        begin(n + 1)
                    store_table(n)

                act.wait_ge(sum0_added, groups_before(0, 0))
                begin(0)
                for m in range(NODES_PER):
                    tile(m, 0, m)
                with act.Fori(1, NT // NODES_PER - 1) as i:
                    for m in range(NODES_PER):
                        tile(NODES_PER * i + m, i, m)
                for m in range(NODES_PER):
                    tile(NT - NODES_PER + m, NT // NODES_PER - 1, m)
            with act.Else():
                act.wait_ge(layer0_summed, 1)
                begin(0)
                dense(0)
                store_table(0)
                with act.Fori(1, NT - 1) as n:
                    begin(n)
                    dense(n)
                    store_table(n)
                begin(NT - 1)
                dense(NT - 1)
                store_table(NT - 1)

            def split_hi(g, q, i):
                act.wait_ge(edge_in[q], 32 * (i + 1))
                if not (static(g) and g < 2):
                    act.wait_ge(z_ready, GROUP * (g - 1))
                act.activation(edge_r[:, q, :], edge_f[:, q, :], ACT.Copy).then_inc(edge_hi, 1)

            split_hi(0, 0, 0)
            split_hi(1, 1, 0)

            def stage_batch(b):
                act.activation(f_sum[:, b % 2, :, :], sumT1[:, :, b * BATCH * T:(b + 1) * BATCH * T],
                               ACT.Copy).then_inc(sum_staged, 1)

            def deviation(h, b):
                act.wait_ge(fvar_ready[h], BATCH * (b + 1))
                act.activation(f_std[0:T, h, in_batch(b), :], f_mv[0:T, h, in_batch(b), 1:2], ACT.Sqrt,
                               bias=eps[0:T, 0:1]).then_inc(fstd_ready[h], 1)

            def norm(h, n, ready):
                act.activation(f_x[0:T, n, :], f_x[0:T, n, :], ACT.Identity, scale=f_rstd[0:T, h, n, :],
                               bias=f_shift[0:T, h, n, :]).then_inc(ready, 1)

            def layer1(windows):
                def keep(s):
                    act.wait_ge(sum1_ready, s + 1)
                    if not (static(s) and s == 0):
                        act.wait_ge(sum1_turned, s)
                    act.activation(sum_rows[:, :], bank[6][0:WIN, 0:D], ACT.Copy).then_inc(sum1_kept, 1)

                def tick(k, i):
                    at = group_at(k, i, -GROUP)
                    if at and not (static(at[0]) and at[0] < 2):
                        split_hi(*at, i + (k + GROUP) // (2 * GROUP))
                    if at := tile_at(k, i, 1):
                        t, ten, _, _ = at
                        act.wait_ge(pre_ready, t + 1)
                        gate = rows[:, ten, D:2 * D]
                        act.activation(gate, gate, ACT.Sigmoid).then_inc(gate_ready, 1)
                    if at := tile_at(k, i, 5):
                        t, ten, five, _ = at
                        if (at := group_at(k, i, 5)) and not (static(at[0]) and at[0] < 2):
                            act.wait_ge(sum1_ready, (at[0] - 1) * windows)
                        act.wait_ge(msg_ready, t + 1)
                        act.activation(msg_hi[:, ten, :], msg[:, five, :], ACT.Copy).then_inc(msg_hi_ready, 1)
                    if at := tile_at(k, i, 1):
                        t, _, five, two = at
                        act.wait_ge(turned, t + 1)
                        if not (static(t) and t < GROUP):
                            act.wait_ge(core_ready, t - (GROUP - 1))
                        act.activation(h_hi[:, five, :], bank[2 + two][:, 0:D], ACT.Relu).then_inc(hi_ready, 1)
                    if windows == 1:
                        if at := group_at(k, i, 11):
                            keep(at[0])
                    elif at := group_at(k, i, 11):
                        g, q = at
                        settle(act)
                        if static(g) and g == 0:
                            keep(0)
                        with act.Fori(1 if static(g) and g == 0 else 0, windows) as w:
                            keep(g * windows + w)
                    if windows == 1 and static(i) and i == PAIRS:
                        for b, when in ((0, 5), (1, 8)):
                            if k == when:
                                act.wait_ge(sum1_added, groups_before(b, BATCH - 1))
                                stage_batch(b)
                        if k == 13:
                            deviation(0, 0)

                ticks(act, tick)
                if windows > 1:
                    act.wait_ge(layer1_summed, 1)
                    stage_batch(0)
                    stage_batch(1)
                    deviation(0, 0)

            with act.If(widest < WIN):
                layer1(1)
            with act.Else():
                layer1(NWIN)

            for time in batch_times(3):
                if (b := batch_at(time, -1)) is not None and b >= 2:
                    if b == 2:
                        act.wait_ge(layer1_summed, 1)
                    act.wait_ge(sum_turned, BATCH * (b - 1))
                    stage_batch(b)
                if (b := batch_at(time, 0)) is not None and b >= 1:
                    deviation(0, b)
                if (b := batch_at(time, 3)) is not None:
                    act.wait_ge(fshift_ready[1], b + 1)
                    for n in range(BATCH * b, BATCH * b + BATCH // 2):
                        norm(1, n, out_by_act)
                if (b := batch_at(time, 2)) is not None:
                    deviation(1, b)
                if (b := batch_at(time, 0)) is not None:
                    act.wait_ge(fshift_ready[0], b + 1)
                    for n in range(BATCH * b, BATCH * (b + 1)):
                        norm(0, n, normed)

        @block.tensor
        def _(pe):
            pe.wait_ge(ident_set, 1)
            pe.wait_ge(ext_ready, 2)
            for s in range(2):
                pe.transpose(bank[s][0:G, 0:P], ext[:, s, 0:G], ident[:, :]).then_inc(ext_turned, 1)
            pe.wait_ge(wide_ready, 2)
            for s in range(2):
                pe.matmul(bank[2 + s][:, 0:G], ext_wide[0:G, s, :], ident[0:G, 0:G]).then_inc(plan_wide, 1)
            pe.wait_ge(plan_ready, 2)
            widest = pe.value_load(span_i[0:1, 0:1], min_val=0, max_val=N)

            T = NODE_TILE

            def mix_x(n):
                pe.wait_ge(xT_in, 16 * (n + 1))
                if static(n) and n == 0:
                    pe.wait_ge(weights_in, 16 * 16)
                else:
                    pe.wait_ge(x1_ready, n)
                pe.matmul(bank[0][0:T, 0:D], ones_f[0:1, 0:T], bias0_row[0:1, :], start=True, stop=False)
                for c in range(C):
                    pe.matmul(bank[0][0:T, c * P:(c + 1) * P], xT_s[:, c, :], ident[:, :],
                              start=False, stop=False, skip_group_check=True)
                for c in range(C):
                    pe.matmul(bank[0][0:T, 0:D], xT_s[:, c, :], loop_sb[:, c, :], start=False, stop=False)

            def mix_sums(n, half):
                if half == 0:
                    pe.wait_ge(staged, n + 1)
                for k in range(half * KB // 2, (half + 1) * KB // 2):
                    last = pe.matmul(bank[0][0:T, 0:D], stage[:, k, :], basis_sb[:, k, :], start=False,
                                     stop=(k == KB - 1))
                if half == 1:
                    last.then_inc(mixed, 1)

            def turn_x1(n):
                pe.wait_ge(x1_ready, n + 1)
                if not (static(n) and n == 0):
                    pe.wait_ge(x1T_ready, n)
                for c in range(C):
                    last = pe.transpose(bank[1][:, c * T:(c + 1) * T], x1_s[0:T, c * P:(c + 1) * P], ident[0:T, 0:T])
                last.then_inc(x1_turned, 1)

            def table(n):
                pe.wait_ge(x1T_ready, n + 1)
                if not (static(n) and n == 0):
                    pe.wait_ge(table_ready, n)
                for c in range(C):
                    last = pe.matmul(bank[2][0:T, :], x1T[:, c, :], wx[:, c, :], start=(c == 0), stop=(c == C - 1))
                last.then_inc(table_mm, 1)

            def layer0(windows):
                def step(q, slot, s, first):
                    pe.wait_ge(whot_ready, s + 1)
                    if not first:
                        pe.wait_ge(sum0_added, s - 1)
                    for c in range(C):
                        for j in range(GROUP):
                            last = pe.matmul(bank[5 + slot][:, c * NB * WIN:(c + 1) * NB * WIN],
                                             x_rows[:, q * GROUP + j, c * P:(c + 1) * P],
                                             whot[:, slot, j, :, :].rearrange("p b w -> p (b w)"),
                                             start=(j == 0), stop=(j == GROUP - 1))
                    last.then_inc(sum0_ready, 1)

                def group(q, g, i):
                    pe.wait_ge(x_in[q], 16 * GROUP * (i + 1))
                    if windows == 1:
                        step(q, slot0(q), g, static(g) and g < 2)
                        return
                    first = static(g) and g == 0
                    settle(pe)
                    if first:
                        for w in range(2):
                            step(q, w, w, True)
                    with pe.Fori(1 if first else 0, windows // 2 - 1) as w:
                        for v in range(2):
                            step(q, v, g * windows + 2 * w + v, False)
                    step(q, 0, g * windows + windows - 2, False)
                    step(q, 1, g * windows + windows - 1, False)

                def time(u, i):
                    if at := group0_at(u, i):
                        group(at[1], at[0], PERIOD // RING0 * i + u // RING0)
                    for lag, work in ((0, mix_x), (1, lambda n: mix_sums(n, 0)),
                                      (2, lambda n: mix_sums(n, 1)), (4, turn_x1), (5, table)):
                        if (n := node0_at(u, i, lag)) is not None:
                            work(n)

                def whole(n):
                    mix_x(n)
                    mix_sums(n, 0)
                    mix_sums(n, 1)
                    turn_x1(n)
                    table(n)

                if windows == 1:
                    periods(pe, time)
                else:
                    rounds(pe, RING0, group)
                    whole(0)
                    with pe.Fori(1, NT) as n:
                        whole(n)

            with pe.If(widest < WIN):
                layer0(1)
            with pe.Else():
                layer0(NWIN)

            pe.wait_ge(split_w, 6)

            def turn_sums(n):
                for c in range(C):
                    at = n % 2 * D + c * P
                    last = pe.transpose(pair_bank(n // 2)[:, at:at + P],
                                        f_sum[:, n // BATCH % 2, c, n % BATCH * T:(n % BATCH + 1) * T], ident[:, :])
                last.then_inc(sum_turned, 1)

            def layer1(windows):
                def sum_tile(q, slot, j):
                    for part in (msg_hi, msg_lo):
                        last = pe.matmul(bank[6][0:WIN, 0:D], hot_r[:, slot, j, :], part[:, q * GROUP + j, :],
                                         start=(j == 0 and part is msg_hi),
                                         stop=(j == GROUP - 1 and part is msg_lo))
                    if j == GROUP - 1:
                        last.then_inc(sum1_ready, 1)

                def begin(s):
                    pe.wait_ge(hot1_ready, s + 1)
                    if not (static(s) and s == 0):
                        pe.wait_ge(sum1_kept, s)

                def sums(q, slot, s):
                    begin(s)
                    for j in range(GROUP):
                        sum_tile(q, slot, j)

                def turn(s):
                    pe.wait_ge(sum1_kept, s + 1)
                    if not (static(s) and s == 0):
                        pe.wait_ge(sum1_added, s)
                    settle(pe)
                    for c in range(C):
                        last = pe.transpose(bank[7][:, c * WIN:(c + 1) * WIN], sum_rows[:, c * P:(c + 1) * P],
                                            ident[0:WIN, 0:WIN])
                    last.then_inc(sum1_turned, 1)

                def edge_products(k, i, lag):
                    t, ten, five, two = tile_at(k, i, lag)
                    if at := group_at(k, i, lag):
                        pe.wait_ge(edge_split, 2 * (at[0] + 1))
                    if not (static(t) and t < 2):
                        pe.wait_ge(pre_ready, t - 1)
                    lhs = edge_r[:, ten // GROUP, five * P:(five + 1) * P]
                    pe.matmul(bank[two][:, :], lhs, we_hi[:, :], start=True, stop=False)
                    pe.matmul(bank[two][:, :], lhs, we_lo[:, :], start=False, stop=True).then_inc(z_ready, 1)

                def tick(k, i):
                    if at := tile_at(k, i, 1):
                        t, ten, _, two = at
                        pe.wait_ge(pre_ready, t + 1)
                        if not (static(t) and t < 2):
                            pe.wait_ge(lo_ready, t - 1)
                        for c in range(C):
                            last = pe.transpose(bank[2 + two][:, c * P:(c + 1) * P],
                                                rows[:, ten, c * P:(c + 1) * P], ident[:, :])
                        last.then_inc(turned, 1)
                    if tile_at(k, i, -1):
                        edge_products(k, i, -1)
                    if at := tile_at(k, i, 3):
                        t, _, five, two = at
                        pe.wait_ge(lo_ready, t + 1)
                        if not (static(t) and t < 2):
                            pe.wait_ge(msg_ready, t - 1)
                        to = bank[4 + two][:, 0:D]
                        pe.matmul(to, ones_r[:, :], b2_r[:, :], start=True, stop=False)
                        for c in range(C):
                            part = slice(c * P, (c + 1) * P)
                            pe.matmul(to, h_hi[:, five, part], w2_hi[:, c, :], start=False, stop=False)
                            pe.matmul(to, h_hi[:, five, part], w2_lo[:, c, :], start=False, stop=False)
                            last = pe.matmul(to, h_lo[:, five, part], w2_hi[:, c, :], start=False, stop=(c == C - 1))
                        last.then_inc(core_ready, 1)
                    at = tile_at(k, i, 7)
                    if windows == 1 and at:
                        t, ten, five, _ = at
                        g, q = 2 * i + (k - 7 - five) // GROUP, ten // GROUP
                        if five == 0:
                            begin(g)
                        if five % 2 == 0:
                            pe.wait_ge(lo_by_pool, 3 * g + five // 2 + 1)
                        else:
                            pe.wait_ge(lo_by_dve, 2 * g + five // 2 + 1)
                        sum_tile(q, q, five)
                    if windows > 1 and (at := group_at(k, i, 11)):
                        g, q = at
                        pe.wait_ge(lo_by_pool, 3 * (g + 1))
                        pe.wait_ge(lo_by_dve, 2 * (g + 1))
                        settle(pe)
                        first = static(g) and g == 0
                        if first:
                            for w in range(2):
                                sums(q, w, w)
                                turn(w)
                        with pe.Fori(1 if first else 0, windows // 2) as w:
                            for v in range(2):
                                sums(q, v, g * windows + 2 * w + v)
                                turn(g * windows + 2 * w + v)
                    if windows == 1 and (at := group_at(k, i, 13)):
                        turn(at[0])
                    if windows == 1 and static(i) and i == PAIRS and 8 <= k < 8 + BATCH:
                        if k == 8:
                            pe.wait_ge(sum_staged, 1)
                            pe.wait_ge(pre_ready, TILES)
                        turn_sums(k - 8)

                edge_products(0, 0, 0)
                ticks(pe, tick)
                if windows > 1:
                    pe.wait_ge(sum_staged, 1)
                    pe.wait_ge(pre_ready, TILES)
                    for n in range(BATCH):
                        turn_sums(n)

            with pe.If(widest < WIN):
                layer1(1)
            with pe.Else():
                layer1(NWIN)

            for b in range(1, BATCHES):
                pe.wait_ge(sum_staged, b + 1)
                if b >= 3:
                    pe.wait_ge(y_ready, BATCH // 2 * (b - 2))
                for n in range(BATCH * b, BATCH * (b + 1)):
                    turn_sums(n)

        @block.vector
        def _(dve):
            dve.memset(zero[:, :], 0.0).then_inc(consts, 1)
            dve.memset(b2_two[:, :], 0.0).then_inc(consts, 1)
            dve.memset(ones_r[:, :].bitcast(F32), 1.0).then_inc(consts, 1)
            dve.memset(eps[:, :], EPS).then_inc(consts, 1)
            dve.memset(ones_f[:, :], 1.0).then_inc(consts, 1)
            for k in range(2):
                dve.memset(sumT0[:, k, :], 0.0).then_inc(sums_zero, 1)
            dve.wait_ge(edges_in, 48)
            dve.tensor_copy(dst_f[:, :], dst_i[:, :]).then_inc(floats_ready, 1)
            dve.tensor_copy(typ_f[:, :], typ_i[:, :]).then_inc(floats_ready, 1)
            dve.tensor_copy(comp_T[:, :, :], comp_bc[:, :].rearrange("p (r b) -> p b r", r=NR)).then_inc(comp_turned, 1)
            dve.wait_ge(floats_ready, 2)
            by_group = dst_f[:, :].rearrange("p (g j) -> p g j", j=GROUP)
            dve.tensor_reduce(ext[:, 0, 0:G], by_group, AX.X, ALU.min).then_inc(ext_ready, 1)
            dve.tensor_reduce(ext[:, 1, 0:G], by_group, AX.X, ALU.max).then_inc(ext_ready, 1)
            dve.wait_ge(ext_turned, 2)
            dve.tensor_reduce(ext2[0:G, 0:1], bank[0][0:G, 0:P], AX.X, ALU.min).then_inc(ext2_ready, 1)
            dve.tensor_reduce(ext2[0:G, 1:2], bank[1][0:G, 0:P], AX.X, ALU.max).then_inc(ext2_ready, 1)
            dve.wait_ge(ext2_ready, 2)
            dve.tensor_tensor(ext2[0:G, 2:3], ext2[0:G, 1:2], ext2[0:G, 0:1], ALU.subtract).then_inc(span_ready, 1)
            dve.wait_ge(span_ready, 1)
            dve.tensor_copy(ext_wide[0:G, 0, :], ext2[0:G, 0:1].to_broadcast([G, P])).then_inc(wide_ready, 1)
            dve.tensor_copy(ext_wide[0:G, 1, :], ext2[0:G, 2:3].to_broadcast([G, P])).then_inc(wide_ready, 1)
            dve.wait_ge(plan_wide, 2)
            dve.tensor_copy(base_row[0:1, 0:G], bank[2][0:1, 0:G]).then_inc(plan_ready, 1)
            dve.tensor_tensor(dst_rel[:, :].rearrange("p (g j) -> p g j", j=GROUP), by_group,
                              bank[2][:, 0:G].rearrange("p (g o) -> p g o", o=1).to_broadcast([P, G, GROUP]),
                              ALU.subtract).then_inc(rel_ready, 1)
            dve.tensor_reduce(span_f[0:1, 0:1], bank[3][0:1, 0:G], AX.X, ALU.max).then_inc(widest_ready, 1)
            dve.wait_ge(iota_set, 1)
            dve.tensor_copy(iota[:, :], iota_i[:, :]).then_inc(iota_ready, 1)
            dve.wait_ge(iota_ready, 1)
            for i in range(G // PERIOD):
                first = i * NODES_PER * NODE_TILE
                rounds_of = PERIOD // RING0
                dve.tensor_tensor(
                    late[0:1, i * PERIOD:(i + 1) * PERIOD].rearrange("p (r q) -> p r q", q=RING0),
                    iota[0:1, first:first + (rounds_of - 1) * NODE_TILE + 1:NODE_TILE].rearrange(
                        "p (r o) -> p r o", o=1).to_broadcast([1, rounds_of, RING0]),
                    bank[2][0:1, i * PERIOD:(i + 1) * PERIOD].rearrange("p (r q) -> p r q", q=RING0),
                    ALU.subtract).then_inc(late_ready, 1)
            dve.wait_ge(late_ready, G // PERIOD)
            dve.tensor_reduce(late_f[0:1, 0:1], late[0:1, :], AX.X, ALU.max).then_inc(late_max_ready, 1)
            dve.wait_ge(late_max_ready, 1)
            dve.tensor_scalar(late_f[0:1, 1:2], late_f[0:1, 0:1], float(NODE_TILE), float(WIN), ALU.is_gt,
                              ALU.mult).then_inc(late_flag_ready, 1)
            dve.wait_ge(late_flag_ready, 1)
            dve.wait_ge(widest_ready, 1)
            dve.tensor_tensor(span_i[0:1, 0:1], span_f[0:1, 0:1], late_f[0:1, 1:2], ALU.max).then_inc(plan_ready, 1)
            dve.wait_ge(rel_ready, 1)
            dve.wait_ge(comp_turned, 1)
            dve.wait_ge(plan_ready, 2)
            widest = dve.value_load(span_i[0:1, 0:1], min_val=0, max_val=N)
            dve.wait_ge(sums_zero, KB)

            def base_of(g):
                at = base_row[0:1, g:g + 1] if static(g) else base_row[0:1, bass.ds(g, 1)]
                return dve.value_load(at, min_val=0, max_val=NPAD - WIN)

            def make_hot(to, g, window, ready):
                shape = [P, GROUP, WIN]
                ends, first = (dst_rel, 0) if window is None else (dst_f, window * WIN)
                return dve.tensor_tensor(
                    to,
                    ends[:, bass.ds(g * GROUP, GROUP)].rearrange("p (j o) -> p j o", o=1).to_broadcast(shape),
                    iota[:, bass.ds(first, WIN)].rearrange("p (o w) -> p o w", o=1).to_broadcast(shape),
                    ALU.is_equal).then_inc(ready, 1)

            def layer0(windows):
                def comp_of_edges(g):
                    dve.tensor_tensor(
                        type_hot[:, :, :],
                        typ_f[:, bass.ds(g * GROUP, GROUP)].rearrange(
                            "p (j o) -> p j o", o=1).to_broadcast([P, GROUP, NR]),
                        iota[:, 0:NR].rearrange("p (o r) -> p o r", o=1).to_broadcast([P, GROUP, NR]),
                        ALU.is_equal).then_inc(type_hot_ready, 1)
                    dve.wait_ge(type_hot_ready, g + 1)
                    shape = [P, GROUP, NB, NR]
                    dve.tensor_tensor(
                        comp_prod[:, :, :, :],
                        type_hot[:, :, :].rearrange("p j (o r) -> p j o r", o=1).to_broadcast(shape),
                        comp_T[:, :, :].rearrange("p (o b) r -> p o b r", o=1).to_broadcast(shape),
                        ALU.mult).then_inc(comp_prod_ready, 1)
                    dve.wait_ge(comp_prod_ready, g + 1)
                    dve.tensor_reduce(comp_e[:, :, :], comp_prod[:, :, :, :], AX.X, ALU.add).then_inc(comp_e_ready, 1)
                    dve.wait_ge(comp_e_ready, g + 1)

                def weigh(slot, g, s, window, first):
                    make_hot(hot[:, :, :], g, window, hot0_ready)
                    dve.wait_ge(hot0_ready, s + 1)
                    if not first:
                        dve.wait_ge(sum0_ready, s - 1)
                    shape = [P, GROUP, NB, WIN]
                    dve.tensor_tensor(
                        whot[:, slot, :, :, :],
                        hot[:, :, :].rearrange("p j (o w) -> p j o w", o=1).to_broadcast(shape),
                        comp_e[:, :, :].rearrange("p j (b o) -> p j b o", o=1).to_broadcast(shape),
                        ALU.mult).then_inc(whot_ready, 1)

                def add(slot, s, base):
                    dve.wait_ge(sum0_ready, s + 1)
                    if not (static(s) and s == 0):
                        dve.wait_ge(sum0_added, s)
                    to = sumT0[:, :, bass.ds(base, WIN)]
                    dve.tensor_tensor(to, to, bank[5 + slot][:, 0:KB * WIN].rearrange("p (k w) -> p k w", k=KB),
                                      ALU.add).then_inc(sum0_added, 1)

                def release_rows():
                    dve.sem_inc(x_used, 1)

                if windows == 1:
                    def time(u, i):
                        if at := group0_at(u, i):
                            g, q = at
                            comp_of_edges(g)
                            weigh(slot0(q), g, g, None, static(g) and g < 2)
                        if not static(i) or 0 < PERIOD * i + u <= G:
                            g = PERIOD * i + u
                            add(slot0(u - 1), g - 1, base_of(g - 1))
                            release_rows()
                        if u == 8 and static(i) and i == 0:
                            split_weights()
                        for lag, work in ((3, variance0), (4, norm0), (5, add_beta), (6, table)):
                            if (n := node0_at(u, i, lag)) is not None:
                                work(n)
                        if u == 0 and static(i) and i == G // PERIOD:
                            dve.wait_ge(sum0_added, G)
                            dve.sem_inc(layer0_summed, 1)

                    periods(dve, time)
                else:
                    def group(q, g, i):
                        comp_of_edges(g)
                        settle(dve)
                        first = static(g) and g == 0
                        if first:
                            for w in range(2):
                                weigh(w, g, w, w, True)
                                add(w, w, w * WIN)
                        with dve.Fori(1 if first else 0, windows // 2) as w:
                            for v in range(2):
                                s = g * windows + 2 * w + v
                                weigh(v, g, s, 2 * w + v, False)
                                add(v, s, (2 * w + v) * WIN)
                        release_rows()

                    def whole(n):
                        variance0(n)
                        norm0(n)
                        add_beta(n)
                        table(n)

                    split_weights()
                    rounds(dve, RING0, group)
                    dve.wait_ge(sum0_added, G * windows)
                    dve.sem_inc(layer0_summed, 1)
                    whole(0)
                    with dve.Fori(1, NT) as n:
                        whole(n)

            def split_weights():
                dve.wait_ge(weights_in, 16 * 16)
                dve.wait_ge(b2_in, 16)
                dve.tensor_copy(we_hi[:, :], we[:, :]).then_inc(w_hi, 1)
                dve.tensor_copy(w2_hi[:, :, :], w2[:, :, :]).then_inc(w_hi, 1)
                dve.tensor_copy(b2_r[:, :], b2_two[:, :]).then_inc(w_hi, 1)
                dve.wait_ge(w_hi, 3)
                dve.tensor_tensor(we_lo[:, :], we[:, :], we_hi[:, :].bitcast(F32), ALU.subtract).then_inc(split_w, 2)
                dve.tensor_tensor(w2_lo[:, :, :], w2[:, :, :], w2_hi[:, :, :].bitcast(F32),
                                  ALU.subtract).then_inc(split_w, 2)
                dve.tensor_tensor(b2_r[32:33, :], b2_two[32:33, :], b2_r[32:33, :].bitcast(F32),
                                  ALU.subtract).then_inc(split_w, 2)

            T = NODE_TILE

            def variance0(n):
                dve.wait_ge(mixed, n + 1)
                dve.bn_stats(stats[0:T, :], bank[0][0:T, 0:D]).then_inc(stats_ready, 1)
                dve.wait_ge(stats_ready, n + 1)
                settle(dve)
                dve.bn_aggr(mv[0:T, :], stats[0:T, :]).then_inc(var_ready, 1)

            def norm0(n):
                dve.wait_ge(std_ready, n + 1)
                dve.reciprocal(rstd[0:T, :], std[0:T, :]).then_inc(rstd_ready, 1)
                if not (static(n) and n == 0):
                    dve.wait_ge(x1_out, 16 * n)
                    dve.wait_ge(x1_turned, n)
                dve.wait_ge(rstd_ready, n + 1)
                dve.tensor_scalar(x1_s[0:T, :], bank[0][0:T, 0:D], mv[0:T, 0:1], rstd[0:T, 0:1], ALU.subtract,
                                  ALU.mult).then_inc(x1_ready, 1)

            def add_beta(n):
                if not (static(n) and n == 0):
                    dve.wait_ge(xb_out, 16 * n)
                dve.wait_ge(x1_ready, n + 1)
                dve.tensor_tensor(xb_s[0:T, :], x1_s[0:T, :], beta_bc[0:T, :], ALU.add).then_inc(xb_ready, 1)

            def table(n):
                dve.wait_ge(table_mm, n + 1)
                if not (static(n) and n == 0):
                    dve.wait_ge(table_out, 16 * n)
                dve.tensor_tensor(table_s[0:T, :], bank[2][0:T, :], bx_bc[0:T, :], ALU.add).then_inc(table_ready, 1)

            with dve.If(widest < WIN):
                layer0(1)
            with dve.Else():
                layer0(NWIN)
            dve.wait_ge(sums_zero, KB + C)

            def split_lo(g, q, half):
                dve.wait_ge(edge_hi, g + 1)
                at = slice(half * GE // 2, (half + 1) * GE // 2)
                dve.tensor_tensor(edge_r[DE:P, q, at], edge_f[DE:P, q, at], edge_r[DE:P, q, at].bitcast(F32),
                                  ALU.subtract).then_inc(edge_split, 1)

            def add_x1(b):
                for pair in range(BATCH // 2 * b, BATCH // 2 * (b + 1)):
                    dve.wait_ge(sum_turned, 2 * (pair + 1))
                    two = f_x[0:T, 2 * pair:2 * pair + 2, :].rearrange("p n d -> p (n d)")
                    dve.tensor_tensor(two, pair_bank(pair), two, ALU.add).then_inc(y_ready, 1)

            def variance(h, b):
                if h == 0:
                    dve.wait_ge(y_ready, BATCH // 2 * (b + 1))
                for n in range(BATCH * b, BATCH * (b + 1)):
                    dve.bn_stats(f_stats[0:T, n % BATCH, :], f_x[0:T, n, :]).then_inc(fstats_ready[h], 1)
                for n in range(BATCH * b, BATCH * (b + 1)):
                    dve.wait_ge(fstats_ready[h], n + 1)
                    dve.bn_aggr(f_mv[0:T, h, n, :], f_stats[0:T, n % BATCH, :]).then_inc(fvar_ready[h], 1)

            def scale_and_shift(h, b):
                batch = in_batch(b)
                dve.wait_ge(fstd_ready[h], b + 1)
                dve.reciprocal(f_rstd[0:T, h, batch, :], f_std[0:T, h, batch, :]).then_inc(frstd_ready[h], 1)
                dve.wait_ge(frstd_ready[h], b + 1)
                dve.scalar_tensor_tensor(out=f_shift[0:T, h, batch, :], in0=f_mv[0:T, h, batch, 0:1], scalar=-1.0,
                                         in1=f_rstd[0:T, h, batch, :], op0=ALU.mult,
                                         op1=ALU.mult).then_inc(fshift_ready[h], 1)

            def layer1(windows):
                split_lo(0, 0, 0)
                split_lo(0, 0, 1)

                def hot1(slot, g, s, window, first):
                    if not first:
                        dve.wait_ge(sum1_ready, s - 1)
                    make_hot(hot_r[:, slot, :, :], g, window, hot1_ready)

                def add(s, base):
                    dve.wait_ge(sum1_turned, s + 1)
                    if not (static(s) and s == 0):
                        dve.wait_ge(sum1_added, s)
                    to = sumT1[:, :, bass.ds(base, WIN)]
                    dve.tensor_tensor(to, to, bank[7][:, 0:C * WIN].rearrange("p (c w) -> p c w", c=C),
                                      ALU.add).then_inc(sum1_added, 1)

                def tick(k, i):
                    for half, ahead in ((0, 4), (1, 2)):
                        if at := group_at(k, i, -ahead):
                            split_lo(*at, half)
                    if at := tile_at(k, i, 0):
                        t, ten, _, two = at
                        dve.wait_ge(row_in[ten], 16 * (i + 1))
                        dve.wait_ge(z_ready, t + 1)
                        row = rows[:, ten, :]
                        dve.tensor_tensor(row, bank[two][:, :], row, ALU.add).then_inc(pre_ready, 1)
                    added = group_at(k, i, 15) if windows == 1 else None
                    if added:
                        base = base_of(added[0])
                    if at := tile_at(k, i, 2):
                        t, _, five, two = at
                        dve.wait_ge(hi_ready, t + 1)
                        dve.scalar_tensor_tensor(out=h_lo[:, five, :], in0=bank[2 + two][:, 0:D], scalar=0.0,
                                                 in1=h_hi[:, five, :].bitcast(F32), op0=ALU.max,
                                                 op1=ALU.subtract).then_inc(lo_ready, 1)
                    if at := tile_at(k, i, 4):
                        t, ten, five, two = at
                        if not (static(t) and t < GROUP):
                            g = 2 * i + (k - 4 - five) // GROUP
                            if five % 2 == 0:
                                dve.wait_ge(lo_by_pool, 3 * (g - 1) + five // 2 + 1)
                            else:
                                dve.wait_ge(lo_by_dve, 2 * (g - 1) + five // 2 + 1)
                        dve.wait_ge(gate_ready, t + 1)
                        dve.wait_ge(core_ready, t + 1)
                        dve.tensor_tensor(msg[:, five, :], rows[:, ten, D:2 * D], bank[4 + two][:, 0:D],
                                          ALU.mult).then_inc(msg_ready, 1)
                    at = tile_at(k, i, 6)
                    if at and at[2] % 2 == 1:
                        t, ten, five, _ = at
                        dve.wait_ge(msg_hi_ready, t + 1)
                        dve.tensor_tensor(msg_lo[:, ten, :], msg[:, five, :], msg_hi[:, ten, :].bitcast(F32),
                                          ALU.subtract).then_inc(lo_by_dve, 1)
                    if windows == 1:
                        if at := group_at(k, i, 5):
                            g, q = at
                            hot1(q, g, g, None, static(g) and g < 2)
                        if added:
                            add(added[0], base)
                    elif at := group_at(k, i, 11):
                        g, q = at
                        settle(dve)
                        first = static(g) and g == 0
                        if first:
                            for w in range(2):
                                hot1(w, g, w, w, True)
                                add(w, w * WIN)
                        with dve.Fori(1 if first else 0, windows // 2) as w:
                            for v in range(2):
                                s = g * windows + 2 * w + v
                                hot1(v, g, s, 2 * w + v, False)
                                add(s, (2 * w + v) * WIN)

                    if windows == 1 and static(i) and i == PAIRS:
                        if k == 11:
                            dve.wait_ge(x1_in, 16)
                            add_x1(0)
                        if k == 12:
                            variance(0, 0)
                        if k == 14:
                            scale_and_shift(0, 0)

                ticks(dve, tick)
                dve.wait_ge(sum1_added, G * windows)
                dve.sem_inc(layer1_summed, 1)
                if windows > 1:
                    dve.wait_ge(x1_in, 16)
                    add_x1(0)
                    variance(0, 0)
                    scale_and_shift(0, 0)

            with dve.If(widest < WIN):
                layer1(1)
            with dve.Else():
                layer1(NWIN)

            dve.wait_ge(xb_in, 16)
            for time in batch_times(3):
                if (b := batch_at(time, 0)) is not None and b >= 1:
                    add_x1(b)
                    variance(0, b)
                if (b := batch_at(time, 3)) is not None:
                    scale_and_shift(1, b)
                if (b := batch_at(time, 2)) is not None:
                    dve.wait_ge(fz_ready, b + 1)
                    scaled = f_x[0:T, in_batch(b), :]
                    dve.tensor_tensor(scaled, scaled, f_xb[0:T, in_batch(b), :], ALU.add).then_inc(fr_ready, 1)
                    dve.wait_ge(fr_ready, b + 1)
                    variance(1, b)
                if (b := batch_at(time, 0)) is not None and b >= 1:
                    scale_and_shift(0, b)


def kernel(x, src, dst, edge_attr_64, edge_type_8, L0_gnn_basis, L0_gnn_comp, L0_gnn_loop_weight,
           L0_gnn_bias_param, L1_gnn_W1, L1_gnn_b1, L1_gnn_W2, L1_gnn_b2, L1_gnn_Wg, L1_gnn_bg,
           L1_gnn_gamma, L1_gnn_beta):
    import numpy as np
    import concourse.bacc as bacc
    from concourse.bass_utils import run_bass_kernel_spmd

    x = np.asarray(x)
    N, D = x.shape
    E = np.asarray(src).shape[0]
    tiles = E // P

    def laid(a):
        return np.ascontiguousarray(np.asarray(a))

    arrays = {
        "x": laid(x),
        "xT": laid(x.T.reshape(D // P, P, N).transpose(1, 0, 2)),
        "src": laid(np.asarray(src).reshape(tiles // GROUP, GROUP, P).transpose(0, 2, 1)),
        "dst": laid(np.asarray(dst).reshape(tiles, P).T),
        "etype": laid(np.asarray(edge_type_8).reshape(tiles, P).T),
        "edge_T": laid(np.asarray(edge_attr_64).T),
        "basis": laid(L0_gnn_basis), "comp": laid(L0_gnn_comp), "loop_w": laid(L0_gnn_loop_weight),
        "bias0": laid(L0_gnn_bias_param), "W1": laid(L1_gnn_W1), "b1": laid(L1_gnn_b1), "W2": laid(L1_gnn_W2),
        "b2": laid(L1_gnn_b2), "Wg": laid(L1_gnn_Wg), "bg": laid(L1_gnn_bg), "gamma": laid(L1_gnn_gamma),
        "beta": laid(L1_gnn_beta),
    }
    nc = bacc.Bacc("TRN2", target_bir_lowering=False, num_devices=1)
    args = {name: nc.dram_tensor(f"in_{name}", a.shape, mybir.dt.from_np(a.dtype), kind="ExternalInput").ap()
            for name, a in arrays.items()}
    out = nc.dram_tensor("out_rows", [N, D], F32, kind="ExternalOutput").ap()
    build(nc, **args, out=out)
    r = run_bass_kernel_spmd(nc, [{f"in_{name}": a for name, a in arrays.items()}], core_ids=[0])
    return r.results[0]["out_rows"]
```
